# Optimizing a Trainium2 kernel written in Bass

```python
import numpy as np
import jax
import jax.numpy as jnp

def _softmax(x, axis=-1):
    return jax.nn.softmax(x, axis=axis)

def _gelu(x):
    return jax.nn.gelu(x, approximate=True)

def _silu(x):
    return jax.nn.silu(x)

def _sigmoid(x):
    return jax.nn.sigmoid(x)

def _layernorm(x, axis=-1, eps=1e-05):
    m = jnp.mean(x, axis=axis, keepdims=True)
    v = jnp.var(x, axis=axis, keepdims=True)
    return (x - m) / jnp.sqrt(v + eps)

def _scatter_add(tgt, idx, src, axis=0):
    return tgt.at[idx].add(src)

def _segment_sum(src, seg, n):
    return jax.ops.segment_sum(src, seg, n)
kernel_name = 'mk_macaron_d1_jaxref_r8_394cdf'

def setup_inputs(seed: int=0):
    np.random.seed(seed)
    _w = jnp.asarray

    def _L0_attn_setup():
        import jax, jax.numpy as jnp
        import numpy as np
        B, S, E = (2, 256, 256)
        NQ, NKV, HD = (16, 4, 128)
        WINDOW = 64
        ROPE_BASE = 10000.0

        def _rope(x):
            half = HD // 2
            freqs = 1.0 / ROPE_BASE ** (2.0 * jnp.arange(half, dtype=jnp.float32) / HD)
            pos = jnp.arange(x.shape[2], dtype=jnp.float32)
            ang = pos[:, None] * freqs[None, :]
            cos = jnp.cos(ang)[None, None].astype(x.dtype)
            sin = jnp.sin(ang)[None, None].astype(x.dtype)
            xe = x[..., 0::2]
            xo = x[..., 1::2]
            re = xe * cos - xo * sin
            ro = xe * sin + xo * cos
            return jnp.stack([re, ro], axis=-1).reshape(x.shape)
        key = jax.random.key(seed)
        ks = jax.random.split(key, 9)
        s_in = 1.0 / np.sqrt(E)
        s_out = 1.0 / np.sqrt(NQ * HD)
        return {'x': jax.random.normal(ks[0], (B, S, E), jnp.float32), 'Wq': jax.random.normal(ks[1], (E, NQ * HD), jnp.float32) * s_in, 'bq': jax.random.normal(ks[2], (NQ * HD,), jnp.float32) * 0.01, 'Wk': jax.random.normal(ks[3], (E, NKV * HD), jnp.float32) * s_in, 'bk': jax.random.normal(ks[4], (NKV * HD,), jnp.float32) * 0.01, 'Wv': jax.random.normal(ks[5], (E, NKV * HD), jnp.float32) * s_in, 'bv': jax.random.normal(ks[6], (NKV * HD,), jnp.float32) * 0.01, 'Wo': jax.random.normal(ks[7], (NQ * HD, E), jnp.float32) * s_out, 'bo': jax.random.normal(ks[8], (E,), jnp.float32) * 0.01}
    _L0_attn_in = _L0_attn_setup()

    def _L0_ffn_setup():
        import jax, jax.numpy as jnp
        import numpy as np
        LN_EPS = 1e-05
        Q_EPS = 1e-05

        def ternary_quantize(w):
            scale = jnp.mean(jnp.abs(w))
            return jnp.clip(jnp.round(w / (scale + Q_EPS)), -1.0, 1.0)

        def layernorm(x, gamma, beta):
            mu = jnp.mean(x, axis=-1, keepdims=True)
            var = jnp.mean(jnp.square(x - mu), axis=-1, keepdims=True)
            return (x - mu) * jax.lax.rsqrt(var + LN_EPS) * gamma + beta
        key = jax.random.key(seed)
        k_x, k_w = jax.random.split(key)
        B, S, D_IN, D_OUT = (4, 256, 256, 256)
        x = jax.random.normal(k_x, (B, S, D_IN), dtype=jnp.float32)
        std = np.sqrt(2.0 / D_OUT).astype(np.float32)
        weight = jax.random.normal(k_w, (D_OUT, D_IN), dtype=jnp.float32) * std
        bias = jnp.zeros((D_OUT,), dtype=jnp.float32)
        ln_gamma = jnp.ones((D_IN,), dtype=jnp.float32)
        ln_beta = jnp.zeros((D_IN,), dtype=jnp.float32)
        return {'x': x, 'weight': weight, 'bias': bias, 'ln_gamma': ln_gamma, 'ln_beta': ln_beta}
    _L0_ffn_in = _L0_ffn_setup()
    _d = {'L0_attn_x': _L0_attn_in['x'], 'L0_attn_Wq': _L0_attn_in['Wq'], 'L0_attn_bq': _L0_attn_in['bq'], 'L0_attn_Wk': _L0_attn_in['Wk'], 'L0_attn_bk': _L0_attn_in['bk'], 'L0_attn_Wv': _L0_attn_in['Wv'], 'L0_attn_bv': _L0_attn_in['bv'], 'L0_attn_Wo': _L0_attn_in['Wo'], 'L0_attn_bo': _L0_attn_in['bo'], 'L0_ffn_weight': _L0_ffn_in['weight'], 'L0_ffn_bias': _L0_ffn_in['bias'], 'L0_ffn_ln_gamma': _L0_ffn_in['ln_gamma'], 'L0_ffn_ln_beta': _L0_ffn_in['ln_beta']}
    _x0 = _d['L0_attn_x']
    _d['L0_attn_x'] = jax.random.normal(jax.random.fold_in(jax.random.key(seed), 1), (8, 512, 256), dtype=_x0.dtype)
    del _x0
    return _d

def reference(L0_attn_x, L0_attn_Wq, L0_attn_bq, L0_attn_Wk, L0_attn_bk, L0_attn_Wv, L0_attn_bv, L0_attn_Wo, L0_attn_bo, L0_ffn_weight, L0_ffn_bias, L0_ffn_ln_gamma, L0_ffn_ln_beta):

    def _L0_attn_ref(x, Wq, bq, Wk, bk, Wv, bv, Wo, bo):
        import jax, jax.numpy as jnp
        import numpy as np
        B, S, E = (2, 256, 256)
        NQ, NKV, HD = (16, 4, 128)
        WINDOW = 64
        ROPE_BASE = 10000.0

        def _rope(x):
            half = HD // 2
            freqs = 1.0 / ROPE_BASE ** (2.0 * jnp.arange(half, dtype=jnp.float32) / HD)
            pos = jnp.arange(x.shape[2], dtype=jnp.float32)
            ang = pos[:, None] * freqs[None, :]
            cos = jnp.cos(ang)[None, None].astype(x.dtype)
            sin = jnp.sin(ang)[None, None].astype(x.dtype)
            xe = x[..., 0::2]
            xo = x[..., 1::2]
            re = xe * cos - xo * sin
            ro = xe * sin + xo * cos
            return jnp.stack([re, ro], axis=-1).reshape(x.shape)
        b, s, _ = x.shape
        q = (x @ Wq + bq).reshape(b, s, NQ, HD).transpose(0, 2, 1, 3)
        k = (x @ Wk + bk).reshape(b, s, NKV, HD).transpose(0, 2, 1, 3)
        v = (x @ Wv + bv).reshape(b, s, NKV, HD).transpose(0, 2, 1, 3)
        q = _rope(q)
        k = _rope(k)
        rep = NQ // NKV
        k = jnp.repeat(k, rep, axis=1)
        v = jnp.repeat(v, rep, axis=1)
        scores = jnp.einsum('bhqd,bhkd->bhqk', q, k) / np.sqrt(HD)
        i = jnp.arange(s)[:, None]
        j = jnp.arange(s)[None, :]
        allowed = (j <= i) & (i - j <= WINDOW)
        scores = jnp.where(allowed[None, None], scores, -jnp.inf)
        weights = jax.nn.softmax(scores, axis=-1)
        out = jnp.einsum('bhqk,bhkd->bhqd', weights, v)
        out = out.transpose(0, 2, 1, 3).reshape(b, s, NQ * HD)
        return out @ Wo + bo

    def _L0_ffn_ref(x, weight, bias, ln_gamma, ln_beta):
        import jax, jax.numpy as jnp
        import numpy as np
        LN_EPS = 1e-05
        Q_EPS = 1e-05

        def ternary_quantize(w):
            scale = jnp.mean(jnp.abs(w))
            return jnp.clip(jnp.round(w / (scale + Q_EPS)), -1.0, 1.0)

        def layernorm(x, gamma, beta):
            mu = jnp.mean(x, axis=-1, keepdims=True)
            var = jnp.mean(jnp.square(x - mu), axis=-1, keepdims=True)
            return (x - mu) * jax.lax.rsqrt(var + LN_EPS) * gamma + beta
        xn = layernorm(x, ln_gamma, ln_beta)
        w_q = ternary_quantize(weight)
        return jnp.einsum('bsi,oi->bso', xn, w_q) + bias
    x = L0_attn_x
    x = x + 0.5 * _L0_ffn_ref(_layernorm(x, axis=-1), L0_ffn_weight, L0_ffn_bias, L0_ffn_ln_gamma, L0_ffn_ln_beta)
    x = x + _L0_attn_ref(_layernorm(x, axis=-1), L0_attn_Wq, L0_attn_bq, L0_attn_Wk, L0_attn_bk, L0_attn_Wv, L0_attn_bv, L0_attn_Wo, L0_attn_bo)
    x = x + 0.5 * _L0_ffn_ref(_layernorm(x, axis=-1), L0_ffn_weight, L0_ffn_bias, L0_ffn_ln_gamma, L0_ffn_ln_beta)
    return x

_drawn_inputs = setup_inputs


def setup_inputs(seed=0):
    import zlib

    import numpy as np

    out = dict(_drawn_inputs(seed))
    spreads = {'L0_ffn_bias': (0.0, 0.713), 'L0_ffn_ln_gamma': (1.0, 0.2), 'L0_ffn_ln_beta': (0.0, 0.1)}
    factors = {'L0_attn_bq': 185.203, 'L0_attn_bk': 200.0, 'L0_attn_bv': 43.673, 'L0_attn_bo': 46.051}
    for name, (base, spread) in spreads.items():
        noise = np.random.default_rng([zlib.crc32(name.encode()), seed]).standard_normal(out[name].shape)
        drawn = base * np.exp(spread * noise) if base else spread * noise
        out[name] = jnp.asarray(drawn.astype(out[name].dtype))
    for name, factor in factors.items():
        out[name] = (out[name] * factor).astype(out[name].dtype)
    return out
```

```python
from contextlib import ExitStack

import numpy as np

import concourse.bass as bass
from concourse import mybir

F32 = mybir.dt.float32
F32R = mybir.dt.float32r
BF16 = mybir.dt.bfloat16
ALU = mybir.AluOpType
ACT = mybir.ActivationFunctionType
AX = mybir.AxisListType

P = 128
BATCHES, SEQ, E = 8, 512, 256
NQ, NKV, HD = 16, 4, 128
WINDOW = 64
ROPE_BASE = 10000.0
LN_EPS = 1e-5
Q_EPS = 1e-5
MASKED = -1e30

GROUP = NQ // NKV
CHUNK = WINDOW
BLOCKS = SEQ // P
EC = E // P
UNITS = NKV * BLOCKS
HALF = HD // 2

JOBS = [
    [("K", 1, "cur"), ("Q", 4, "cur")],
    [("Q", 5, "cur"), ("Q", 6, "cur")],
    [("Q", 7, "cur"), ("V", (1, 0), "cur")],
    [("V", (1, 1), "cur")],
    [("K", 2, "cur"), ("Q", 8, "cur")],
    [("Q", 9, "cur"), ("Q", 10, "cur"), ("YT", 0, "prev")],
    [("Q", 11, "cur"), ("FO", 0, "prev"), ("YT", 1, "prev")],
    [("FO", 1, "prev"), ("YT", 0, "next")],
    [("K", 3, "cur"), ("Q", 12, "cur"), ("Q", 13, "cur")],
    [("FO", 0, "next"), ("YT", 1, "next"), ("Q", 14, "cur")],
    [("FO", 1, "next"), ("Q", 15, "cur")],
    [("XT", 0, "next"), ("XT", 1, "next")],
    [("K", 0, "next"), ("Q", 0, "next")],
    [("Q", 1, "next"), ("Q", 2, "next")],
    [("Q", 3, "next"), ("V", (0, 0), "next")],
    [("V", (0, 1), "next")],
]


class Phase:

    def __init__(self, name, b):
        self.name, self.b, self.parts = name, b, PARTS[name]

    def has(self, part):
        return part in self.parts

    def jobs(self, j):
        return [x for x in JOBS[j] if x[2] in self.parts]

    def unit(self, j, lag):
        exists = self.has("cur") if j >= lag else self.has("prev")
        return UNITS * self.b + (j - lag) if exists else None


PARTS = {
    "prologue": ("next",),
    "first": ("cur", "next"),
    "middle": ("prev", "cur", "next"),
    "last": ("prev", "cur"),
    "epilogue": ("prev",),
}
ORDER = list(PARTS)
MIDDLES = BATCHES - 2
ALL_JOBS = [x for row in JOBS for x in row]
NORMS = [("norm2", 0, "prev"), ("norm1", 0, "next"), ("norm_attn", 0, "next")]


class Tally:

    def __init__(self, items, weight):
        self.items, self.weight = items, weight

    def in_pass(self, name):
        return sum(self.weight(x) for x in self.items if x[2] in PARTS[name])

    def start(self, phase):
        n = sum(self.in_pass(name) * (MIDDLES if name == "middle" else 1)
                for name in ORDER[:ORDER.index(phase.name)])
        return n + (phase.b - 1) * self.in_pass("middle") if phase.name == "middle" else n

    def before(self, phase, item):
        held = [x for x in self.items if x[2] in phase.parts]
        return self.start(phase) + sum(self.weight(x) for x in held[:held.index(item)])

    def after(self, phase, item):
        return self.before(phase, item) + self.weight(item)

    def parity(self, phase, item):
        assert self.in_pass("middle") % 2 == 0
        return self.before(Phase(phase.name, 1), item) % 2


def of(*kinds):
    return lambda x: int(x[0] in kinds)


BANKED = Tally(ALL_JOBS, lambda x: 1)
BY_KIND = {kind: Tally(ALL_JOBS, of(kind)) for kind in ("V", "YT", "FO", "XT")}
ROPED = Tally(ALL_JOBS, of("Q", "K"))
VALUES = BY_KIND["V"]
FFN_IN = BY_KIND["YT"]
FFN_OUT = BY_KIND["FO"]
XN = BY_KIND["XT"]
Y_HALVES = Tally(ALL_JOBS, of("YT", "XT"))
SHIFTS = Tally(ALL_JOBS, lambda x: int(x[0] == "V" and x[1][1] == 1))
BIASED = {part: Tally(ALL_JOBS, lambda x, part=part: int(x[0] == "YT" and x[2] == part)) for part in ("prev", "next")}
NORMED = Tally(NORMS, lambda x: 1)
NORM_STEPS = Tally(NORMS, lambda x: 1 if x[0] == "norm_attn" else 6)


def last_in_bank(phase, x):
    earlier = {"first": "prologue", "middle": "first", "last": "first", "epilogue": "last"}
    held = [y for y in ALL_JOBS if y[2] in phase.parts]
    if phase.name in earlier:
        held = [y for y in ALL_JOBS if y[2] in PARTS[earlier[phase.name]]] + held
    at = len(held) - 1 - held[::-1].index(x)
    if at < 2:
        return None, None
    was, between = held[at - 2], held[at - 1]
    tally = ROPED if was[0] in ("Q", "K") else BY_KIND[was[0]]
    return was, tally.before(phase, x) - tally.weight(between)


def block_kernel(nc, x, wq, bq, wk, bk, wv, bv, wo, bo, ffn_wT, ffn_b, gamma, beta,
                 cosT, sinT, mask, ident_bf, ident, out):
    x_t = x.rearrange("b (k p) e -> b p k e", p=P)
    out_t = out.rearrange("b (k p) e -> b p k e", p=P)

    with ExitStack() as ctx:
        def sb(name, shape, dt=F32):
            return ctx.enter_context(nc.sbuf_tensor(name, shape, dt))

        def psum(name, shape, dt=F32):
            return ctx.enter_context(nc.psum_tensor(name, shape, dt))

        def sem(name):
            return ctx.enter_context(nc.semaphore(name))

        wq_s = sb("wq_s", [P, 2, EC, NQ * HD], F32R)
        wk_s = sb("wk_s", [P, 2, EC, NKV * HD], F32R)
        wv_s = sb("wv_s", [P, 2, EC, NKV * HD], F32R)
        wo_s = sb("wo_s", [P, 2, NQ, E], F32R)
        w_tern = sb("w_tern", [P, EC, E], F32R)
        xnT = sb("xnT", [P, 2, EC, SEQ], F32R)
        lnT = sb("lnT", [P, 2, EC, 2 * P], F32R)
        ln_full = sb("ln_full", [P, EC, 2 * P])
        q_s = sb("q_s", [P, 2, 2, SEQ // CHUNK, GROUP, CHUNK], F32R)
        k_s = sb("k_s", [P, 2, 2, SEQ], F32R)
        v_s = sb("v_s", [P, 2, BLOCKS, NKV * HD], F32R)
        v_odd = sb("v_odd", [P, 2, BLOCKS - 1, NKV * HD], F32R)
        probs = sb("probs", [P, 2, 4, P])
        probsT = sb("probsT", [P, 2, 2, GROUP * CHUNK], F32R)
        headsT = sb("headsT", [P, 2, GROUP, 2, CHUNK], F32R)
        neg_max = sb("neg_max", [P, 2, 4])
        row_sum = sb("row_sum", [P, 2, 4])
        inv_sum = sb("inv_sum", [P, 2, 4])
        rope_cos = sb("rope_cos", [P, 2, SEQ])
        rope_sin = sb("rope_sin", [P, 2, SEQ])
        cos_t = sb("cos_t", [P, SEQ])
        sin_t = sb("sin_t", [P, SEQ])
        x_in = sb("x_in", [P, BLOCKS, E])
        x_mid = sb("x_mid", [P, BLOCKS, E])
        x_res = sb("x_res", [P, BLOCKS, E])
        y = sb("y", [P, 2, E])
        half_b = sb("half_b", [P, E])
        bo_t = sb("bo_t", [P, E])
        mask_s = sb("mask_s", [P, 6 * P], BF16)
        identb = sb("identb", [P, P], BF16)
        identf = sb("identf", [P, P])
        bq_s = sb("bq_s", [P, NQ])
        bk_s = sb("bk_s", [P, NKV])
        bv_s = sb("bv_s", [P, NKV])
        gamma_s = sb("gamma_s", [P, EC])
        beta_s = sb("beta_s", [P, EC])
        parts = sb("parts", [P, BLOCKS, 6])
        stats = sb("stats", [P, BLOCKS, 2])
        sums = sb("sums", [P, 4, BLOCKS])
        tmp = sb("tmp", [P, 5, BLOCKS])
        rstd = sb("rstd", [P, BLOCKS])
        minus_half = sb("minus_half", [P, BLOCKS])
        eps = sb("eps", [P, BLOCKS])
        thr = sb("thr", [P, 4])

        scores_p = [psum(f"scores_p{i}", [P, 4, P]) for i in range(2)]
        probsT_p = psum("probsT_p", [P, 4, P])
        heads_p = psum("heads_p", [P, GROUP, 2, CHUNK])
        job_p = [psum(f"job_p{i}", [P, SEQ]) for i in range(2)]
        attn_p = [psum(f"attn_p{i}", [P, 2, E]) for i in range(2)]

        consts_in = sem("consts_in")
        tern_in = sem("tern_in")
        rows_in = sem("rows_in")
        x_loaded = sem("x_loaded")
        out_stored = sem("out_stored")
        staged = [sem(f"staged{i}") for i in range(4)]
        split_hi = sem("split_hi")
        split_lo = sem("split_lo")
        v_shifted = sem("v_shifted")
        ones_ready = sem("ones_ready")
        abs_summed = sem("abs_summed")
        scale_ready = sem("scale_ready")
        thr_step = sem("thr_step")
        tern_ready = sem("tern_ready")
        bias_ready = sem("bias_ready")
        power_ready = sem("power_ready")

        scores_ready = sem("scores_ready")
        max_ready = sem("max_ready")
        exp_ready = sem("exp_ready")
        inv_ready = sem("inv_ready")
        probs_ready = sem("probs_ready")
        probsT_ready = sem("probsT_ready")
        probsT_hi = sem("probsT_hi")
        probsT_lo = sem("probsT_lo")
        heads_ready = sem("heads_ready")
        heads_hi = sem("heads_hi")
        heads_lo = sem("heads_lo")
        projected = sem("projected")
        attn_read = sem("attn_read")

        job_ready = sem("job_ready")
        job_read_dve = sem("job_read_dve")
        job_read_act = sem("job_read_act")
        rope_swapped = sem("rope_swapped")
        rope_cosed = sem("rope_cosed")
        rope_sined = sem("rope_sined")
        rope_added = sem("rope_added")
        rope_hi = sem("rope_hi")
        rope_lo = sem("rope_lo")
        v_hi = sem("v_hi")
        v_lo = sem("v_lo")
        ln_hi = sem("ln_hi")
        ln_scaled = sem("ln_scaled")
        ln_lo = sem("ln_lo")
        xn_hi = sem("xn_hi")
        xn_lo = sem("xn_lo")
        ffn_added = sem("ffn_added")
        parts_ready = sem("parts_ready")
        gathered = sem("gathered")
        stats_ready = sem("stats_ready")
        rstd_step = sem("rstd_step")
        rstd_ready = sem("rstd_ready")
        y_ready = sem("y_ready")
        biased = {part: sem(f"biased_{part}") for part in ("prev", "next")}
        res_ready = sem("res_ready")

        def quarter(w, i):
            return w.rearrange("(c p) n -> p c n", p=P)[:, :, i * SEQ:(i + 1) * SEQ]

        def heads_of(i):
            return wo.rearrange("(h d) n -> d h n", d=HD)[:, i * GROUP:(i + 1) * GROUP, :]

        def part_of(t, i):
            return [t[:, s, :, i * SEQ:(i + 1) * SEQ] for s in range(2)]

        def wo_part(i):
            return [wo_s[:, s, i * GROUP:(i + 1) * GROUP, :] for s in range(2)]

        stage_c = rope_cos[:, :, :]
        stage_s = rope_sin[:, :, :]
        stage_r = x_res[:, :, :].rearrange("p k e -> p (k e)").rearrange("p (c n) -> p c n", c=2)
        stage_rh = x_res[:, :, :]
        stage_p = probs[:, :, :, :].rearrange("p a k n -> p a (k n)")
        stage_ph = probs[:, :, :, :].rearrange("p a k n -> p (a k n)").rearrange("p (h n) -> p h n", h=GROUP)
        PIECES = [
            (stage_c, 0, quarter(wk, 0), part_of(wk_s, 0)),
            (stage_s, 1, quarter(wq, 0), part_of(wq_s, 0)),
            (stage_r, 2, quarter(wv, 0), part_of(wv_s, 0)),
            (stage_p, 3, quarter(wq, 1), part_of(wq_s, 1)),
            (stage_ph, 3, heads_of(0), wo_part(0)),
            (stage_r, 2, quarter(wq, 2), part_of(wq_s, 2)),
            (stage_rh, 2, heads_of(1), wo_part(1)),
            (stage_r, 2, quarter(wq, 3), part_of(wq_s, 3)),
            (stage_rh, 2, heads_of(2), wo_part(2)),
            (stage_rh, 2, heads_of(3), wo_part(3)),
        ]
        LATE = {1: (6,), 3: (7,), 5: (8,), 6: (9,)}
        NEEDS = {"K": lambda i: 0, "V": lambda i: 2, "Q": lambda i: (1, 3, 5, 7)[i // GROUP]}
        WO_PIECE = (4, 6, 8, 9)

        def staged_before(n):
            return [i for i in range(n) if PIECES[i][1] == PIECES[n][1]]

        def passes(eng):
            yield Phase("prologue", -1)
            yield Phase("first", 0)
            with eng.Fori(1, BATCHES - 1) as b:
                yield Phase("middle", b)
            yield Phase("last", BATCHES - 1)
            yield Phase("epilogue", BATCHES)

        def bank_of(phase, x):
            return job_p[BANKED.parity(phase, x)]

        def roped(x, s):
            kind, i, _ = x
            return q_s[:, (i // GROUP) % 2, s, :, i % GROUP, :] if kind == "Q" else k_s[:, i % 2, s, :]

        def as_roped(x, ap):
            return ap.rearrange("p (c q) -> p c q", q=CHUNK) if x[0] == "Q" else ap

        def v_part(i, s):
            half, m = i
            width = NKV * HD // 2
            return v_s[:, s, 2 * m:2 * m + 2, half * width:(half + 1) * width]

        def xn_part(m, s):
            return xnT[:, s, :, 2 * P * m:2 * P * (m + 1)]

        def rope_tasks(phase, j):
            tasks, open_ = [], None
            for i in range(j + 1):
                heads = [x for x in phase.jobs(i) if x[0] in ("Q", "K")]
                for x in phase.jobs(i):
                    if i == j:
                        tasks.append(("take", x))
                    if x in heads:
                        if open_ and i == j:
                            tasks.append(("end", open_))
                        open_ = x
                if open_ and not heads:
                    if i == j:
                        tasks.append(("end", open_))
                    open_ = None
            return tasks

        def pieces(phase, j):
            if phase.name == "prologue":
                return {11: (0, 1, 2), 12: (3,), 14: (4,), 15: (5,)}.get(j, ())
            return LATE.get(j, ()) if phase.name == "first" else ()

        block = ctx.enter_context(nc.Block())

        @block.sync
        def _(sp):
            def load_x(b):
                sp.dma_start(x_in[:, :, :], x_t[b]).then_inc(x_loaded, 16)

            def stage(n):
                where, s, src, _ = PIECES[n]
                if staged_before(n):
                    sp.wait_ge(split_lo, staged_before(n)[-1] + 1)
                sp.dma_start(where, src).then_inc(staged[s], 16)

            def shift_values(phase, half):
                sp.wait_ge(v_lo, VALUES.after(phase, ("V", (half, 1), "cur" if half else "next")))
                cols = slice(half * NKV * HD // 2, (half + 1) * NKV * HD // 2)
                for s in range(2):
                    sp.dma_start(v_odd[0:CHUNK, s, :, cols].bitcast(F32),
                                 v_s[CHUNK:P, s, 0:BLOCKS - 1, cols].bitcast(F32)).then_inc(v_shifted, 16)
                    sp.dma_start(v_odd[CHUNK:P, s, :, cols].bitcast(F32),
                                 v_s[0:CHUNK, s, 1:BLOCKS, cols].bitcast(F32)).then_inc(v_shifted, 16)

            sp.dma_start(ln_full[:, :, :], ffn_wT.rearrange("(c p) n -> p c n", p=P)).then_inc(tern_in, 16)
            load_x(0)
            for dst, src in ((identf, ident), (gamma_s, gamma), (beta_s, beta), (half_b, ffn_b.partition_broadcast(P)),
                             (bo_t, bo.partition_broadcast(P))):
                sp.dma_start(dst[:, :], src).then_inc(rows_in, 16)
            for n in range(3):
                stage(n)
            for dst, src in ((bq_s, bq), (bk_s, bk), (bv_s, bv), (cos_t, cosT), (sin_t, sinT),
                             (identb, ident_bf), (mask_s, mask)):
                sp.dma_start(dst[:, :], src).then_inc(consts_in, 16)
            stage(3)
            for phase in passes(sp):
                for j in range(UNITS):
                    if phase.name == "prologue" and j in (12, 14):
                        stage({12: 4, 14: 5}[j])
                    if phase.name == "first":
                        for n in LATE.get(j, ()):
                            stage(n)
                    if j == 0 and phase.has("cur") and phase.has("next"):
                        sp.wait_ge(ffn_added, FFN_OUT.start(phase))
                        load_x(phase.b + 1)
                    if j == 3 and phase.has("cur"):
                        shift_values(phase, 1)
                    if j == 7 and phase.has("prev"):
                        sp.wait_ge(ffn_added, FFN_OUT.after(phase, ("FO", 1, "prev")))
                        sp.dma_start(out_t[phase.b - 1], x_res[:, :, :]).then_inc(out_stored, 16)
                    if j == 15 and phase.has("next"):
                        shift_values(phase, 0)
            sp.wait_ge(out_stored, 16 * BATCHES)

        @block.tensor
        def _(pe):
            def three(dst, a, b, first, last, clears):
                for i, (p, q) in enumerate(((0, 0), (0, 1), (1, 0))):
                    mm = nc.tensor.matmul(dst, a(p), b(q), start=first and clears and i == 0,
                                          stop=last and i == 2, skip_group_check=True)
                return mm

            def scores(phase, j):
                u, g, t = phase.unit(j, 0), j // BLOCKS, j % BLOCKS
                if t == 0:
                    pe.wait_ge(rope_lo, ROPED.after(phase, ("Q", GROUP * g + GROUP - 1, "cur")) if g
                               else ROPED.start(phase))
                if not (phase.name == "first" and j < 2):
                    pe.wait_ge(exp_ready, u - 1)
                dst = scores_p[j % 2]
                off = 0 if t == 0 else 2 * P
                nc.tensor.matmul(dst[:, :, :], identb[:, :], mask_s[:, off:off + 4 * P],
                                 start=True, stop=False, skip_group_check=True)
                for cc in range(2):
                    c = 2 * t + cc
                    w0 = CHUNK * max(c - 1, 0)
                    for pair in range(2):
                        mm = three(dst[:, 2 * cc + pair, :],
                                   lambda s: q_s[:, g % 2, s, c, 2 * pair:2 * pair + 2, :],
                                   lambda s: k_s[:, g % 2, s, w0:w0 + P], False, True, False)
                mm.then_inc(scores_ready, 1)

            def project(phase, j):
                u, jj = phase.unit(j, 3), (j - 3) % UNITS
                g, t = jj // BLOCKS, jj % BLOCKS
                pe.wait_ge(heads_lo, u + 1)
                if phase.name == "first" and t == 0:
                    pe.wait_ge(split_lo, WO_PIECE[g] + 1)
                if jj == 0 and phase.has("prev"):
                    pe.wait_ge(attn_read, 2 * phase.b)
                for h in range(GROUP):
                    mm = three(attn_p[t // 2][:, t % 2, :], lambda s: headsT[:, s, h, :, :],
                               lambda s: wo_s[:, s, GROUP * g + h, :],
                               g == 0 and h == 0, g == NKV - 1 and h == GROUP - 1, t % 2 == 0)
                mm.then_inc(projected, 1)

            def values(phase, j):
                u, jj = phase.unit(j, 2), (j - 2) % UNITS
                g, t = jj // BLOCKS, jj % BLOCKS
                pe.wait_ge(probsT_lo, u + 1)
                if jj in (0, UNITS // 2):
                    pe.wait_ge(v_shifted, 64 * (SHIFTS.after(phase, ("V", (1, 1), "cur")) if jj
                                                else SHIFTS.start(phase)))
                for cc in range(2):
                    c = 2 * t + cc
                    src, at = (v_s, max(c - 1, 0) // 2) if c == 0 or c % 2 else (v_odd, c // 2 - 1)
                    mm = three(heads_p[:, :, cc, :], lambda s: src[:, s, at, g * HD:(g + 1) * HD],
                               lambda s: probsT[:, s, cc, :], True, True, cc == 0)
                mm.then_inc(heads_ready, 1)

            def transpose_probs(phase, j):
                u = phase.unit(j, 1)
                pe.wait_ge(probs_ready, u + 1)
                for k in range(4):
                    mm = nc.tensor.transpose(probsT_p[:, k, :], probs[:, (j - 1) % 2, k, :], identf[:, :])
                mm.then_inc(probsT_ready, 1)

            def wait_for_bank(phase, x):
                was, n = last_in_bank(phase, x)
                if was is None:
                    return
                if was[0] in ("Q", "K"):
                    pe.wait_ge(rope_cosed, n)
                elif was[0] == "V":
                    pe.wait_ge(v_lo, n)
                elif was[0] == "YT":
                    pe.wait_ge(ln_scaled, 2 * n)
                elif was[0] == "FO":
                    pe.wait_ge(ffn_added, n)
                elif was[0] == "XT":
                    pe.wait_ge(xn_lo, n)

            def job(phase, x):
                kind, i, _ = x
                bank = bank_of(phase, x)
                wait_for_bank(phase, x)
                if kind in NEEDS and phase.name in ("prologue", "first"):
                    pe.wait_ge(split_lo, NEEDS[kind](i) + 1)
                if x == ("K", 0, "next"):
                    pe.wait_ge(xn_lo, XN.after(phase, ("XT", 1, "next")))
                if kind in ("Q", "K"):
                    w = wq_s if kind == "Q" else wk_s
                    for e in range(EC):
                        mm = three(bank[:, :], lambda s: w[:, s, e, i * HD:(i + 1) * HD],
                                   lambda s: xnT[:, s, e, :], e == 0, e == EC - 1, True)
                if kind == "V":
                    half, m = i
                    width = NKV * HD // 2
                    for k in range(2):
                        at = (2 * m + k) * P
                        for e in range(EC):
                            mm = three(bank[:, k * width:(k + 1) * width], lambda s: xnT[:, s, e, at:at + P],
                                       lambda s: wv_s[:, s, e, half * width:(half + 1) * width],
                                       e == 0, e == EC - 1, k == 0)
                if kind in ("YT", "XT"):
                    pe.wait_ge(y_ready, Y_HALVES.after(phase, x))
                    for e in range(EC):
                        for k in range(2):
                            at = (2 * e + k) * P
                            mm = nc.tensor.transpose(bank[:, at:at + P], y[:, k, e * P:(e + 1) * P], identf[:, :])
                if kind == "FO":
                    pe.wait_ge(ln_lo, FFN_OUT.after(phase, x))
                    for k in range(2):
                        for e in range(EC):
                            for s in range(2):
                                mm = nc.tensor.matmul(bank[:, k * E:(k + 1) * E], lnT[:, s, e, k * P:(k + 1) * P],
                                                      w_tern[:, e, :], start=k == 0 and e == 0 and s == 0,
                                                      stop=e == EC - 1 and s == 1, skip_group_check=True)
                mm.then_inc(job_ready, 1)

            pe.wait_ge(abs_summed, 2)
            nc.tensor.matmul(scores_p[0][:, 0, 0:1], y[:, 0, 0:P], thr[:, 0:1],
                             start=True, stop=True).then_inc(scale_ready, 1)
            pe.wait_ge(rows_in, 16 * 5)
            pe.wait_ge(tern_ready, 1)
            for phase in passes(pe):
                if phase.name == "first":
                    pe.wait_ge(consts_in, 16 * 7)
                for j in range(UNITS):
                    if phase.has("cur"):
                        scores(phase, j)
                    if phase.unit(j, 3) is not None and (j < 3 or phase.has("cur")):
                        project(phase, j)
                    if phase.unit(j, 2) is not None:
                        values(phase, j)
                    for x in phase.jobs(j):
                        job(phase, x)
                    if phase.unit(j, 1) is not None:
                        transpose_probs(phase, j)

        @block.vector
        def _(dve):
            def split_low(n):
                where, _, _, dst = PIECES[n]
                dve.wait_ge(split_hi, n + 1)
                nc.vector.tensor_tensor(dst[1], where, dst[0].bitcast(F32), ALU.subtract).then_inc(split_lo, 1)

            def max_of(phase, j):
                dve.wait_ge(scores_ready, phase.unit(j, 0) + 1)
                nc.vector.tensor_reduce(neg_max[:, j % 2, :], scores_p[j % 2][:, :, :], AX.X, ALU.max,
                                        negate=True).then_inc(max_ready, 1)

            def invert_sums(phase, j):
                dve.wait_ge(exp_ready, phase.unit(j, 0) + 1)
                nc.vector.reciprocal(inv_sum[:, j % 2, :], row_sum[:, j % 2, :]).then_inc(inv_ready, 1)

            def heads_low(phase, j):
                g = (j - 2) % UNITS // BLOCKS
                dve.wait_ge(heads_hi, phase.unit(j, 2) + 1)
                nc.vector.scalar_tensor_tensor(
                    out=headsT[:, 1, :, :, :].rearrange("p h c q -> p (h c q)"), in0=heads_p[:, :, :, :].rearrange("p h c q -> p (h c q)"),
                    scalar=bv_s[:, g:g + 1], in1=headsT[:, 0, :, :, :].rearrange("p h c q -> p (h c q)").bitcast(F32),
                    op0=ALU.add, op1=ALU.subtract).then_inc(heads_lo, 1)

            def probsT_low(phase, j):
                dve.wait_ge(probsT_hi, phase.unit(j, 1) + 1)
                nc.vector.tensor_tensor(probsT[:, 1, :, :], probsT_p[:, :, :].rearrange("p (c a) n -> p c (a n)", c=2),
                                        probsT[:, 0, :, :].bitcast(F32), ALU.subtract).then_inc(probsT_lo, 1)

            def rope_end(phase, x):
                dve.wait_ge(rope_hi, ROPED.after(phase, x))
                nc.vector.tensor_tensor(roped(x, 1), as_roped(x, rope_cos[:, ROPED.parity(phase, x), :]),
                                        roped(x, 0).bitcast(F32), ALU.subtract).then_inc(rope_lo, 1)

            def take(phase, x):
                kind, i, part = x
                bank = bank_of(phase, x)
                halves = "p (k n) -> p k n"
                dve.wait_ge(job_ready, BANKED.after(phase, x))
                if kind in ("Q", "K"):
                    dve.wait_ge(rope_swapped, ROPED.after(phase, x))
                    n = ROPED.before(phase, x)
                    if not (phase.name == "prologue" and n < 2):
                        dve.wait_ge(rope_lo, n - 1)
                    r = ROPED.parity(phase, x)
                    if x == ("K", 0, "next") and phase.name == "prologue":
                        dve.wait_ge(consts_in, 16 * 7)
                    bias = (bq_s if kind == "Q" else bk_s)[:, i:i + 1]
                    nc.vector.scalar_tensor_tensor(
                        out=rope_cos[:, r, :], in0=bank[:, :], scalar=bias, in1=cos_t[:, :],
                        op0=ALU.add, op1=ALU.mult).then_inc(rope_cosed, 1)
                if kind == "V":
                    dve.wait_ge(v_hi, VALUES.after(phase, x))
                    nc.vector.tensor_tensor(v_part(i, 1), bank[:, :].rearrange(halves, k=2), v_part(i, 0).bitcast(F32),
                                            ALU.subtract).then_inc(v_lo, 1)
                if kind == "XT":
                    dve.wait_ge(xn_hi, XN.after(phase, x))
                    nc.vector.tensor_tensor(xn_part(i, 1), bank[:, :].rearrange(halves, k=2),
                                            xn_part(i, 0).bitcast(F32), ALU.subtract).then_inc(xn_lo, 1)
                if kind == "YT":
                    if not (phase.name == "prologue" and i == 0):
                        dve.wait_ge(ln_lo, FFN_IN.before(phase, x))
                    for e in range(EC):
                        nc.vector.tensor_scalar(ln_full[:, e, :], bank[:, e * 2 * P:(e + 1) * 2 * P],
                                                gamma_s[:, e:e + 1], beta_s[:, e:e + 1],
                                                ALU.mult, ALU.add).then_inc(ln_scaled, 1)
                    dve.wait_ge(ln_hi, FFN_IN.after(phase, x))
                    nc.vector.tensor_tensor(lnT[:, 1, :, :], ln_full[:, :, :], lnT[:, 0, :, :].bitcast(F32),
                                            ALU.subtract).then_inc(ln_lo, 1)
                if kind == "FO":
                    src, dst = (x_res, x_res) if part == "prev" else (x_in, x_mid)
                    dve.wait_ge(biased[part], BIASED[part].after(phase, ("YT", i, part)))
                    if part == "next" and phase.has("cur"):
                        dve.wait_ge(res_ready, phase.b + 1)
                    nc.vector.scalar_tensor_tensor(
                        out=dst[:, 2 * i:2 * i + 2, :], in0=bank[:, :].rearrange(halves, k=2), scalar=0.5,
                        in1=src[:, 2 * i:2 * i + 2, :], op0=ALU.mult, op1=ALU.add).then_inc(ffn_added, 1)

            def statistics(phase, norm, src, blocks):
                if not (phase.name == "prologue" and norm == NORMS[1]):
                    dve.wait_ge(stats_ready, NORMED.before(phase, norm))
                for k in blocks:
                    nc.vector.bn_stats(parts[:, k, :], src[:, k, :]).then_inc(parts_ready, 1)

            def gather_statistics(phase, norm):
                done = 5 * NORMED.before(phase, norm)
                dve.wait_ge(parts_ready, BLOCKS * NORMED.after(phase, norm))
                even, odd = parts[:, :, 0:3], parts[:, :, 3:6]
                nc.vector.tensor_tensor(sums[:, 0, :], even[:, :, 1], odd[:, :, 1], ALU.add).then_inc(gathered, 1)
                nc.vector.tensor_tensor(sums[:, 1, :], even[:, :, 1], odd[:, :, 1], ALU.subtract).then_inc(gathered, 1)
                nc.vector.tensor_tensor(sums[:, 2, :], even[:, :, 2], odd[:, :, 2], ALU.add).then_inc(gathered, 1)
                dve.wait_ge(gathered, done + 2)
                nc.vector.tensor_scalar(stats[:, :, 0], sums[:, 0, :], 0.5, None, ALU.mult).then_inc(gathered, 1)
                nc.vector.scalar_tensor_tensor(out=sums[:, 3, :], in0=sums[:, 1, :], scalar=0.25, in1=sums[:, 1, :],
                                               op0=ALU.mult, op1=ALU.mult).then_inc(gathered, 1)
                dve.wait_ge(gathered, done + 5)
                nc.vector.scalar_tensor_tensor(out=stats[:, :, 1], in0=sums[:, 2, :], scalar=1.0 / E,
                                               in1=sums[:, 3, :], op0=ALU.mult, op1=ALU.add).then_inc(stats_ready, 1)

            def normalize(phase, norm, src, m):
                dve.wait_ge(rstd_ready, NORMED.after(phase, norm))
                for k in range(2):
                    at = 2 * m + k
                    ins = nc.vector.tensor_scalar(y[:, k, :], src[:, at, :], stats[:, at, 0:1], rstd[:, at:at + 1],
                                                  ALU.subtract, ALU.mult)
                ins.then_inc(y_ready, 1)

            def after_attention(phase):
                dve.wait_ge(projected, UNITS * phase.b)
                dve.wait_ge(res_ready, phase.b)
                for m in range(2):
                    nc.vector.tensor_tensor(x_res[:, 2 * m:2 * m + 2, :], attn_p[m][:, :, :],
                                            x_res[:, 2 * m:2 * m + 2, :], ALU.add).then_inc(attn_read, 1)

            nc.vector.memset(y[:, 0, 0:P], 1.0).then_inc(abs_summed, 1)
            dve.wait_ge(tern_in, 16)
            nc.vector.tensor_reduce(thr[:, 0:1], ln_full[:, :, :].rearrange("p c n -> p (c n)"), AX.X, ALU.add,
                                    apply_absolute_value=True).then_inc(abs_summed, 1)
            dve.wait_ge(scale_ready, 1)
            nc.vector.tensor_scalar(thr[:, 1:2], scores_p[0][:, 0, 0:1], 1.0 / (E * E), Q_EPS,
                                    ALU.mult, ALU.add).then_inc(thr_step, 1)
            dve.wait_ge(thr_step, 1)
            nc.vector.tensor_scalar(thr[:, 2:3], thr[:, 1:2], 0.5, None, ALU.mult).then_inc(thr_step, 1)
            dve.wait_ge(thr_step, 2)
            nc.vector.tensor_scalar(x_mid[:, 0:2, :], ln_full[:, :, :], thr[:, 2:3], None,
                                    ALU.is_gt).then_inc(thr_step, 1)
            nc.vector.tensor_scalar(x_mid[:, 2:4, :], ln_full[:, :, :], -1.0, thr[:, 2:3],
                                    ALU.mult, ALU.is_gt).then_inc(thr_step, 1)
            dve.wait_ge(thr_step, 4)
            nc.vector.tensor_tensor(w_tern[:, :, :], x_mid[:, 0:2, :], x_mid[:, 2:4, :],
                                    ALU.subtract).then_inc(tern_ready, 1)
            dve.wait_ge(rows_in, 16 * 5)
            for phase in passes(dve):
                for j in range(UNITS):
                    if phase.has("cur"):
                        max_of(phase, j)
                    if j == 3 and phase.has("prev"):
                        after_attention(phase)
                    if phase.unit(j, 2) is not None:
                        heads_low(phase, j)
                    if j == 3 and phase.has("prev"):
                        dve.wait_ge(attn_read, 2 * phase.b)
                        statistics(phase, NORMS[0], x_res, range(BLOCKS))
                        gather_statistics(phase, NORMS[0])
                    if j == 4 and phase.has("prev"):
                        normalize(phase, NORMS[0], x_res, 0)
                    if j == 11 and phase.has("next"):
                        normalize(phase, NORMS[2], x_mid, 0)
                        dve.wait_ge(job_ready, BANKED.after(phase, ("XT", 0, "next")))
                        normalize(phase, NORMS[2], x_mid, 1)
                    tasks = rope_tasks(phase, j)
                    for n in range(max(len(tasks), 1)):
                        if tasks:
                            (take if tasks[n][0] == "take" else rope_end)(phase, tasks[n][1])
                        if n == 0 and phase.has("cur"):
                            invert_sums(phase, j)
                    if j == 5 and phase.has("prev"):
                        normalize(phase, NORMS[0], x_res, 1)
                    if j == 5 and phase.has("next"):
                        dve.wait_ge(x_loaded, 16 * (phase.b + 2))
                        statistics(phase, NORMS[1], x_in, range(BLOCKS))
                        gather_statistics(phase, NORMS[1])
                    if j in (6, 7) and phase.has("next"):
                        normalize(phase, NORMS[1], x_in, j - 6)
                    if j in (9, 10) and phase.has("next"):
                        dve.wait_ge(ffn_added, FFN_OUT.after(phase, ("FO", j - 9, "next")))
                        statistics(phase, NORMS[2], x_mid, range(2 * (j - 9), 2 * (j - 9) + 2))
                    if j == 10 and phase.has("next"):
                        gather_statistics(phase, NORMS[2])
                    for n in pieces(phase, j):
                        split_low(n)
                    if phase.unit(j, 1) is not None:
                        probsT_low(phase, j)

        @block.scalar
        def _(act):
            def split_high(n):
                where, s, _, dst = PIECES[n]
                act.wait_ge(staged[s], 16 * (len(staged_before(n)) + 1))
                nc.scalar.activation(dst[0], where, ACT.Copy).then_inc(split_hi, 1)

            def exp_of(phase, j):
                act.wait_ge(max_ready, phase.unit(j, 0) + 1)
                if phase.name == "first" and j == 0:
                    act.wait_ge(split_lo, WO_PIECE[0] + 1)
                for k in range(4):
                    ins = nc.scalar.activation(probs[:, j % 2, k, :], scores_p[j % 2][:, k, :], ACT.Exp,
                                               bias=neg_max[:, j % 2, k:k + 1], accum_out=row_sum[:, j % 2, k:k + 1])
                ins.then_inc(exp_ready, 1)

            def heads_high(phase, j):
                g = (j - 2) % UNITS // BLOCKS
                act.wait_ge(heads_ready, phase.unit(j, 2) + 1)
                nc.scalar.activation(headsT[:, 0, :, :, :].rearrange("p h c q -> p (h c q)"), heads_p[:, :, :, :].rearrange("p h c q -> p (h c q)"),
                                     ACT.Identity, bias=bv_s[:, g:g + 1]).then_inc(heads_hi, 1)

            def probsT_high(phase, j):
                act.wait_ge(probsT_ready, phase.unit(j, 1) + 1)
                nc.scalar.activation(probsT[:, 0, :, :], probsT_p[:, :, :].rearrange("p (c a) n -> p c (a n)", c=2),
                                     ACT.Copy).then_inc(probsT_hi, 1)

            def rope_end(phase, x):
                kind, i, part = x
                act.wait_ge(rope_added, ROPED.after(phase, x))
                g = (i // GROUP if kind == "Q" else i) + (NKV if part == "next" else 0)
                if phase.has("cur") and not (phase.name == "first" and g == 1):
                    act.wait_ge(scores_ready, UNITS * phase.b + BLOCKS * (g - 1))
                nc.scalar.activation(roped(x, 0), as_roped(x, rope_cos[:, ROPED.parity(phase, x), :]),
                                     ACT.Copy).then_inc(rope_hi, 1)

            def take(phase, x):
                kind, i, part = x
                bank = bank_of(phase, x)
                halves = "p (k n) -> p k n"
                if kind == "FO":
                    return
                act.wait_ge(job_ready, BANKED.after(phase, x))
                if kind in ("Q", "K"):
                    r = ROPED.parity(phase, x)
                    bias = (bq_s if kind == "Q" else bk_s)[:, i:i + 1]
                    if x == ("K", 0, "next") and phase.name == "prologue":
                        act.wait_ge(consts_in, 16 * 7)
                        act.wait_ge(split_lo, 2)
                    n = ROPED.before(phase, x)
                    if not (phase.name == "prologue" and n < 2):
                        act.wait_ge(rope_added, n - 1)
                    nc.scalar.activation(rope_sin[0:HALF, r, :], bank[HALF:P, :], ACT.Identity, bias=bias[HALF:P, :])
                    nc.scalar.activation(rope_sin[HALF:P, r, :], bank[0:HALF, :], ACT.Identity,
                                         bias=bias[0:HALF, :]).then_inc(rope_swapped, 1)
                if kind == "V":
                    if i[0] == 1 and phase.has("prev"):
                        act.wait_ge(heads_ready, UNITS * phase.b)
                    if i[0] == 0 and phase.has("cur"):
                        act.wait_ge(heads_ready, UNITS * phase.b + UNITS // 2)
                    nc.scalar.activation(v_part(i, 0), bank[:, :].rearrange(halves, k=2), ACT.Copy).then_inc(v_hi, 1)
                if kind == "XT":
                    nc.scalar.activation(xn_part(i, 0), bank[:, :].rearrange(halves, k=2), ACT.Copy).then_inc(xn_hi, 1)
                if kind == "YT":
                    act.wait_ge(ln_scaled, 2 * FFN_IN.after(phase, x))
                    nc.scalar.activation(lnT[:, 0, :, :], ln_full[:, :, :], ACT.Copy).then_inc(ln_hi, 1)

            act.wait_ge(rows_in, 16 * 5)
            for phase in passes(act):
                for j in range(UNITS):
                    if phase.has("cur"):
                        exp_of(phase, j)
                    if phase.unit(j, 2) is not None:
                        heads_high(phase, j)
                    for what, x in rope_tasks(phase, j):
                        (take if what == "take" else rope_end)(phase, x)
                    for n in pieces(phase, j):
                        split_high(n)
                    if phase.unit(j, 1) is not None:
                        probsT_high(phase, j)

        @block.gpsimd
        def _(pool):
            def scale_of(phase, norm):
                done = NORM_STEPS.before(phase, norm)
                var = stats[:, :, 1]
                pool.wait_ge(stats_ready, NORMED.after(phase, norm))
                nc.gpsimd.tensor_tensor(tmp[:, 0, :], var, eps[:, :], ALU.add).then_inc(rstd_step, 1)
                pool.wait_ge(rstd_step, done + 1)
                if norm[0] == "norm_attn":
                    nc.gpsimd.tensor_tensor(rstd[:, :], tmp[:, 0, :], minus_half[:, :], ALU.pow).then_inc(rstd_ready, 1)
                    return
                nc.gpsimd.tensor_tensor(tmp[:, 1, :], tmp[:, 0, :], minus_half[:, :], ALU.pow).then_inc(rstd_step, 1)
                pool.wait_ge(rstd_step, done + 2)
                nc.gpsimd.tensor_tensor(tmp[:, 2, :], var, tmp[:, 1, :], ALU.mult).then_inc(rstd_step, 1)
                pool.wait_ge(rstd_step, done + 3)
                nc.gpsimd.tensor_tensor(tmp[:, 3, :], tmp[:, 2, :], tmp[:, 1, :], ALU.mult).then_inc(rstd_step, 1)
                pool.wait_ge(rstd_step, done + 4)
                nc.gpsimd.tensor_tensor(tmp[:, 4, :], tmp[:, 3, :], eps[:, :], ALU.add).then_inc(rstd_step, 1)
                pool.wait_ge(rstd_step, done + 5)
                nc.gpsimd.tensor_tensor(tmp[:, 2, :], tmp[:, 4, :], minus_half[:, :], ALU.pow).then_inc(rstd_step, 1)
                pool.wait_ge(rstd_step, done + 6)
                nc.gpsimd.tensor_tensor(rstd[:, :], tmp[:, 1, :], tmp[:, 2, :], ALU.mult).then_inc(rstd_ready, 1)

            def normalize_probs(phase, j):
                pool.wait_ge(inv_ready, phase.unit(j, 0) + 1)
                nc.gpsimd.tensor_tensor(probs[:, j % 2, :, :], probs[:, j % 2, :, :],
                                        inv_sum[:, j % 2, :].unsqueeze(2).to_broadcast([P, 4, P]),
                                        ALU.mult).then_inc(probs_ready, 1)

            def rope(phase, x):
                r = ROPED.parity(phase, x)
                pool.wait_ge(rope_swapped, ROPED.after(phase, x))
                nc.gpsimd.tensor_tensor(rope_sin[:, r, :], rope_sin[:, r, :], sin_t[:, :], ALU.mult).then_inc(rope_sined, 1)
                pool.wait_ge(rope_sined, ROPED.after(phase, x))
                pool.wait_ge(rope_cosed, ROPED.after(phase, x))
                nc.gpsimd.tensor_tensor(rope_cos[:, r, :], rope_cos[:, r, :], rope_sin[:, r, :], ALU.add).then_inc(rope_added, 1)

            def bias_residual(phase, part, m):
                buf = x_res if part == "prev" else x_in
                pool.wait_ge(y_ready, Y_HALVES.after(phase, ("YT", m, part)))
                nc.gpsimd.tensor_tensor(buf[:, 2 * m:2 * m + 2, :], buf[:, 2 * m:2 * m + 2, :],
                                        half_b[:, :].unsqueeze(1).to_broadcast([P, 2, E]), ALU.add).then_inc(biased[part], 1)

            def residual(phase):
                if phase.has("prev"):
                    pool.wait_ge(out_stored, 16 * phase.b)
                else:
                    pool.wait_ge(split_lo, len(PIECES))
                    pool.wait_ge(ffn_added, FFN_OUT.start(phase))
                nc.gpsimd.tensor_tensor(x_res[:, :, :], x_mid[:, :, :],
                                        bo_t[:, :].unsqueeze(1).to_broadcast([P, BLOCKS, E]), ALU.add).then_inc(res_ready, 1)

            nc.gpsimd.memset(minus_half[:, :], -0.5).then_inc(power_ready, 1)
            nc.gpsimd.memset(eps[:, :], LN_EPS).then_inc(power_ready, 1)
            pool.wait_ge(power_ready, 2)
            pool.wait_ge(rows_in, 16 * 5)
            nc.gpsimd.tensor_scalar(half_b[:, :], half_b[:, :], 0.5, None, ALU.mult).then_inc(bias_ready, 1)
            pool.wait_ge(bias_ready, 1)
            for phase in passes(pool):
                if phase.name == "prologue":
                    pool.wait_ge(x_loaded, 16)
                for j in range(UNITS):
                    taken = [x for x in phase.jobs(j) if x[0] in ("Q", "K")]
                    for n in range(max(len(taken), 1)):
                        if taken:
                            if phase.name == "prologue" and taken[n][:2] == ("K", 0):
                                pool.wait_ge(consts_in, 16 * 7)
                            rope(phase, taken[n])
                        if n == 0 and phase.has("cur"):
                            normalize_probs(phase, j)
                    if j == 3 and phase.has("prev"):
                        scale_of(phase, NORMS[0])
                    if j in (4, 5) and phase.has("prev"):
                        bias_residual(phase, "prev", j - 4)
                    if j == 5 and phase.has("next"):
                        scale_of(phase, NORMS[1])
                    if j in (6, 7) and phase.has("next"):
                        bias_residual(phase, "next", j - 6)
                    if j == 8 and phase.has("cur"):
                        residual(phase)
                    if j == 10 and phase.has("next"):
                        scale_of(phase, NORMS[2])


def constants():
    half = np.arange(HALF, dtype=np.float32)
    freqs = np.float32(1.0) / np.float32(ROPE_BASE) ** (np.float32(2.0) * half / np.float32(HD))
    angles = (np.arange(SEQ, dtype=np.float32)[:, None] * freqs[None, :]).astype(np.float32).T.astype(np.float64)
    scale = float(HD) ** -0.25
    cosT = (np.concatenate([np.cos(angles)] * 2) * scale).astype(np.float32)
    sinT = (np.concatenate([-np.sin(angles), np.sin(angles)]) * scale).astype(np.float32)
    q = np.arange(P)[:, None] % CHUNK
    key = np.arange(P)[None, :]
    windowed = (key - CHUNK <= q) & (q - (key - CHUNK) <= WINDOW)
    causal = key <= q
    mask = np.concatenate([causal] * 2 + [windowed] * 4, axis=1)
    return cosT, sinT, np.where(mask, 0.0, MASKED), np.eye(P)


def kernel(L0_attn_x, L0_attn_Wq, L0_attn_bq, L0_attn_Wk, L0_attn_bk, L0_attn_Wv, L0_attn_bv, L0_attn_Wo,
           L0_attn_bo, L0_ffn_weight, L0_ffn_bias, L0_ffn_ln_gamma, L0_ffn_ln_beta):
    import ml_dtypes
    import concourse.bacc as bacc
    from concourse.bass_utils import run_bass_kernel_spmd

    def evens_first(w):
        w = np.asarray(w)
        heads = w.reshape(*w.shape[:-1], -1, HALF, 2)
        return np.ascontiguousarray(np.swapaxes(heads, -1, -2).reshape(w.shape))

    def by_head(b):
        return np.ascontiguousarray(np.asarray(b).reshape(-1, HD).T)

    cosT, sinT, mask, eye = constants()
    arrays = {
        "x": np.ascontiguousarray(L0_attn_x),
        "wq": evens_first(L0_attn_Wq), "bq": by_head(evens_first(L0_attn_bq)),
        "wk": evens_first(L0_attn_Wk), "bk": by_head(evens_first(L0_attn_bk)),
        "wv": np.ascontiguousarray(L0_attn_Wv), "bv": by_head(L0_attn_bv),
        "wo": np.ascontiguousarray(L0_attn_Wo), "bo": np.ascontiguousarray(L0_attn_bo),
        "ffn_wT": np.ascontiguousarray(np.asarray(L0_ffn_weight).T), "ffn_b": np.ascontiguousarray(L0_ffn_bias),
        "gamma": by_head(L0_ffn_ln_gamma), "beta": by_head(L0_ffn_ln_beta),
        "cosT": cosT, "sinT": sinT, "mask": mask.astype(ml_dtypes.bfloat16),
        "ident_bf": eye.astype(ml_dtypes.bfloat16), "ident": eye.astype(np.float32),
    }
    nc = bacc.Bacc("TRN2", target_bir_lowering=False, num_devices=1)
    args = [nc.dram_tensor(name, a.shape, mybir.dt.from_np(a.dtype), kind="ExternalInput").ap()
            for name, a in arrays.items()]
    out = nc.dram_tensor("out", (BATCHES, SEQ, E), F32, kind="ExternalOutput").ap()
    block_kernel(nc, *args, out)
    r = run_bass_kernel_spmd(nc, [arrays], core_ids=[0])
    return r.results[0]["out"]
```

```python
from contextlib import ExitStack

import numpy as np

import concourse.bass as bass
from concourse import mybir

F32 = mybir.dt.float32
F32R = mybir.dt.float32r
BF16 = mybir.dt.bfloat16
ALU = mybir.AluOpType
ACT = mybir.ActivationFunctionType
AX = mybir.AxisListType

P = 128
BATCHES, SEQ, E = 8, 512, 256
NQ, NKV, HD = 16, 4, 128
WINDOW = 64
ROPE_BASE = 10000.0
LN_EPS = 1e-5
Q_EPS = 1e-5
MASKED = -1e30

GROUP = NQ // NKV
CHUNK = WINDOW
BLOCKS = SEQ // P
EC = E // P
UNITS = NKV * BLOCKS
HALF = HD // 2

TENSOR = """
    K1c Q4c
    S0c O13p W14p T15p Q5c Q6c
    S1c Q7c O14p W15p T0c
    S2c O15p V10c W0c T1c
    S3c K2c V11c O0c W1c Q8c T2c
    S4c O1c W2c YT0p Q9c T3c Q10c
    S5c O2c W3c FO0p T4c YT1p
    S6c Q11c O3c W4c T5c K3c
    S7c O4c FO1p YT0n W5c Q12c T6c Q13c
    S8c O5c W6c T7c
    S9c FO0n YT1n O6c W7c T8c
    S10c O7c FO1n W8c Q14c Q15c T9c
    S11c O8c XT0n W9c T10c XT1n V00n O9c K0n W10c Q0n
    S12c T11c
    S13c O10c W11c Q1n T12c
    S14c Q2n O11c Q3n W12c T13c
    S15c V01n O12c W13c T14c
"""
VECTOR = """
    heads13p K1c probsT14p
    max0c Q4c inv0c end_K1c heads14p Q5c
    max1c probsT15p end_Q4c heads15p Q6c inv1c probsT0c end_Q5c
    max2c evac0p Q7c w6f V10c stats0p heads0c probsT1c inv2c end_Q6c K2c
    max3c V11c end_Q7c heads1c probsT2c inv3c norm0p
    max4c Q8c YT0p w7f end_K2c heads2c inv4c end_Q8c probsT3c end_YT0p norm1p Q9c
    max5c Q10c FO0p w8f heads3c probsT4c YT1p
    max6c inv5c end_YT1p stats0n end_Q9c Q11c heads4c end_Q10c norm0n probsT5c K3c
    max7c inv6c FO1p YT0n end_Q11c inv7c heads5c norm1n probsT6c Q12c
    max8c w9f end_K3c end_YT0n Q13c heads6c inv8c w0i probsT7c YT1n
    max9c end_Q12c FO0n heads7c end_YT1n probsT8c
    max10c inv9c astats0n FO1n astats1n end_Q13c w1i inv10c heads8c anorm0n Q14c probsT9c Q15c
    max11c w2i anorm1n XT0n heads9c XT1n V00n probsT10c w3i end_Q14c end_Q15c inv11c heads10c K0n Q0n
    max12c probsT11c
    max13c inv12c end_K0n inv13c Q1n heads11c probsT12c end_Q0n
    max14c inv14c Q2n heads12c
    max15c end_Q1n w4i probsT13c Q3n end_Q2n V01n inv15c w5i end_Q3n
"""
SCALAR = """
    heads13p K1c Q4c probsT14p
    exp0c heads14p end_K1c Q5c Q6c probsT15p end_Q4c
    exp1c heads15p probsT0c end_Q5c w6f Q7c V10c
    exp2c heads0c probsT1c end_Q6c K2c end_Q7c V11c heads1c
    exp3c probsT2c Q8c end_K2c w7f heads2c
    exp4c YT0p end_Q8c probsT3c Q9c Q10c w8f heads3c probsT4c
    exp5c YT1p end_Q9c Q11c end_Q10c heads4c
    exp6c probsT5c K3c end_Q11c w9f heads5c
    exp7c w0i w1i YT0n probsT6c Q12c Q13c end_K3c
    exp8c heads6c probsT7c end_Q12c YT1n heads7c w2i probsT8c
    exp9c end_Q13c
    exp10c heads8c Q14c probsT9c w3i Q15c XT0n heads9c probsT10c XT1n V00n end_Q14c end_Q15c
    exp11c K0n heads10c Q0n probsT11c
    exp12c end_K0n
    exp13c Q1n heads11c end_Q0n probsT12c Q2n
    exp14c w4i end_Q1n heads12c probsT13c Q3n w5i end_Q2n
    exp15c V01n end_Q3n
"""
GPSIMD = """
    K1c Q4c
    probs0c Q5c
    probs1c Q6c Q7c scale0p
    probs2c K2c
    probs3c Q8c
    probs4c Q9c bias0p Q10c
    probs5c scale0n bias1p Q11c
    probs6c K3c bias0n
    probs7c Q12c bias1n residual0c
    probs8c Q13c
    probs9c ascale0n
    probs10c Q14c Q15c
    probs11c K0n
    probs12c Q0n
    probs13c Q1n Q2n
    probs14c Q3n
    probs15c
"""

SYNC = """
    load0c stage4i stage5i stage6f shift1c stage7f stage8f stage9f store0p shift0n
"""


def steps(table):
    found = []
    for step in table.split():
        name = step[:-1].rstrip("0123456789")
        index = step[len(name):-1]
        found.append((name, (int(index[0]), int(index[1])) if name == "V" else int(index or 0), PART[step[-1]]))
    return found


PART = {"p": "prev", "c": "cur", "n": "next", "i": "prologue", "f": "first"}
JOB_KINDS = ("K", "Q", "V", "YT", "FO", "XT")


class Phase:

    def __init__(self, name, b):
        self.name, self.b, self.parts = name, b, PARTS[name]

    def has(self, part):
        return part in self.parts

    def steps(self, table):
        return [x for x in steps(table) if x[2] in (*self.parts, self.name)]

    def unit(self, x):
        return UNITS * (self.b - (x[2] == "prev")) + x[1]


PARTS = {
    "prologue": ("next",),
    "first": ("cur", "next"),
    "middle": ("prev", "cur", "next"),
    "last": ("prev", "cur"),
    "epilogue": ("prev",),
}
ORDER = list(PARTS)
MIDDLES = BATCHES - 2
ALL_JOBS = [x for x in steps(TENSOR) if x[0] in JOB_KINDS]
NORMS = [("norm2", 0, "prev"), ("norm1", 0, "next"), ("norm_attn", 0, "next")]


class Tally:

    def __init__(self, items, weight):
        self.items, self.weight = items, weight

    def in_pass(self, name):
        return sum(self.weight(x) for x in self.items if x[2] in PARTS[name])

    def start(self, phase):
        n = sum(self.in_pass(name) * (MIDDLES if name == "middle" else 1)
                for name in ORDER[:ORDER.index(phase.name)])
        return n + (phase.b - 1) * self.in_pass("middle") if phase.name == "middle" else n

    def before(self, phase, item):
        held = [x for x in self.items if x[2] in phase.parts]
        return self.start(phase) + sum(self.weight(x) for x in held[:held.index(item)])

    def after(self, phase, item):
        return self.before(phase, item) + self.weight(item)

    def parity(self, phase, item):
        assert self.in_pass("middle") % 2 == 0
        return self.before(Phase(phase.name, 1), item) % 2


def of(*kinds):
    return lambda x: int(x[0] in kinds)


BANKED = Tally(ALL_JOBS, lambda x: 1)
BY_KIND = {kind: Tally(ALL_JOBS, of(kind)) for kind in ("V", "YT", "FO", "XT")}
ROPED = Tally(ALL_JOBS, of("Q", "K"))
VALUES = BY_KIND["V"]
FFN_IN = BY_KIND["YT"]
FFN_OUT = BY_KIND["FO"]
XN = BY_KIND["XT"]
Y_HALVES = Tally(ALL_JOBS, of("YT", "XT"))
SHIFTS = Tally(ALL_JOBS, lambda x: int(x[0] == "V" and x[1][1] == 1))
BIASED = {part: Tally(ALL_JOBS, lambda x, part=part: int(x[0] == "YT" and x[2] == part)) for part in ("prev", "next")}
NORMED = Tally(NORMS, lambda x: 1)
NORM_STEPS = Tally(NORMS, lambda x: 1 if x[0] == "norm_attn" else 6)


def last_in_bank(phase, x):
    earlier = {"first": "prologue", "middle": "first", "last": "first", "epilogue": "last"}
    held = [y for y in ALL_JOBS if y[2] in phase.parts]
    if phase.name in earlier:
        held = [y for y in ALL_JOBS if y[2] in PARTS[earlier[phase.name]]] + held
    at = len(held) - 1 - held[::-1].index(x)
    if at < 2:
        return None, None
    was, between = held[at - 2], held[at - 1]
    tally = ROPED if was[0] in ("Q", "K") else BY_KIND[was[0]]
    return was, tally.before(phase, x) - tally.weight(between)


def block_kernel(nc, x, wq, bq, wk, bk, wv, bv, wo, bo, ffn_wT, ffn_b, gamma, beta,
                 cosT, sinT, mask, ident_bf, ident, out):
    x_t = x.rearrange("b (k p) e -> b p k e", p=P)
    out_t = out.rearrange("b (k p) e -> b p k e", p=P)

    with ExitStack() as ctx:
        def sb(name, shape, dt=F32):
            return ctx.enter_context(nc.sbuf_tensor(name, shape, dt))

        def psum(name, shape, dt=F32):
            return ctx.enter_context(nc.psum_tensor(name, shape, dt))

        def sem(name):
            return ctx.enter_context(nc.semaphore(name))

        wq_s = sb("wq_s", [P, 2, EC, NQ * HD], F32R)
        wk_s = sb("wk_s", [P, 2, EC, NKV * HD], F32R)
        wv_s = sb("wv_s", [P, 2, EC, NKV * HD], F32R)
        wo_s = sb("wo_s", [P, 2, NQ, E], F32R)
        w_tern = sb("w_tern", [P, EC, E], F32R)
        xnT = sb("xnT", [P, 2, EC, SEQ], F32R)
        lnT = sb("lnT", [P, 2, EC, 2 * P], F32R)
        ln_full = sb("ln_full", [P, EC, 2 * P])
        q_s = sb("q_s", [P, 2, 2, SEQ // CHUNK, GROUP, CHUNK], F32R)
        k_s = sb("k_s", [P, 2, 2, SEQ], F32R)
        v_s = sb("v_s", [P, 2, BLOCKS, NKV * HD], F32R)
        v_odd = sb("v_odd", [P, 2, BLOCKS - 1, NKV * HD], F32R)
        probs = sb("probs", [P, 2, 4, P])
        probsT = sb("probsT", [P, 2, 2, GROUP * CHUNK], F32R)
        headsT = sb("headsT", [P, 2, GROUP, 2, CHUNK], F32R)
        neg_max = sb("neg_max", [P, 2, 4])
        row_sum = sb("row_sum", [P, 2, 4])
        inv_sum = sb("inv_sum", [P, 2, 4])
        rope_cos = sb("rope_cos", [P, 2, SEQ])
        rope_sin = sb("rope_sin", [P, 2, SEQ])
        cos_t = sb("cos_t", [P, SEQ])
        sin_t = sb("sin_t", [P, SEQ])
        x_in = sb("x_in", [P, BLOCKS, E])
        x_mid = sb("x_mid", [P, BLOCKS, E])
        x_res = sb("x_res", [P, BLOCKS, E])
        y = sb("y", [P, 2, E])
        half_b = sb("half_b", [P, E])
        bo_t = sb("bo_t", [P, E])
        mask_s = sb("mask_s", [P, 6 * P], BF16)
        identb = sb("identb", [P, P], BF16)
        identf = sb("identf", [P, P])
        bq_s = sb("bq_s", [P, NQ])
        bk_s = sb("bk_s", [P, NKV])
        bv_s = sb("bv_s", [P, NKV])
        gamma_s = sb("gamma_s", [P, EC])
        beta_s = sb("beta_s", [P, EC])
        parts = sb("parts", [P, BLOCKS, 6])
        stats = sb("stats", [P, BLOCKS, 2])
        sums = sb("sums", [P, 4, BLOCKS])
        tmp = sb("tmp", [P, 5, BLOCKS])
        rstd = sb("rstd", [P, BLOCKS])
        minus_half = sb("minus_half", [P, BLOCKS])
        eps = sb("eps", [P, BLOCKS])
        thr = sb("thr", [P, 4])

        scores_p = [psum(f"scores_p{i}", [P, 4, P]) for i in range(2)]
        probsT_p = psum("probsT_p", [P, 4, P])
        heads_p = psum("heads_p", [P, GROUP, 2, CHUNK])
        job_p = [psum(f"job_p{i}", [P, SEQ]) for i in range(2)]
        attn_p = [psum(f"attn_p{i}", [P, 2, E]) for i in range(2)]

        consts_in = sem("consts_in")
        tern_in = sem("tern_in")
        rows_in = sem("rows_in")
        x_loaded = sem("x_loaded")
        out_stored = sem("out_stored")
        staged = [sem(f"staged{i}") for i in range(4)]
        split_hi = sem("split_hi")
        split_lo = sem("split_lo")
        v_shifted = sem("v_shifted")
        ones_ready = sem("ones_ready")
        abs_summed = sem("abs_summed")
        scale_ready = sem("scale_ready")
        thr_step = sem("thr_step")
        tern_ready = sem("tern_ready")
        bias_ready = sem("bias_ready")
        power_ready = sem("power_ready")

        scores_ready = sem("scores_ready")
        max_ready = sem("max_ready")
        exp_ready = sem("exp_ready")
        inv_ready = sem("inv_ready")
        probs_ready = sem("probs_ready")
        probsT_ready = sem("probsT_ready")
        probsT_hi = sem("probsT_hi")
        probsT_lo = sem("probsT_lo")
        heads_ready = sem("heads_ready")
        heads_hi = sem("heads_hi")
        heads_lo = sem("heads_lo")
        projected = sem("projected")
        attn_read = sem("attn_read")

        job_ready = sem("job_ready")
        job_read_dve = sem("job_read_dve")
        job_read_act = sem("job_read_act")
        rope_swapped = sem("rope_swapped")
        rope_cosed = sem("rope_cosed")
        rope_sined = sem("rope_sined")
        rope_added = sem("rope_added")
        rope_hi = sem("rope_hi")
        rope_lo = sem("rope_lo")
        v_hi = sem("v_hi")
        v_lo = sem("v_lo")
        ln_hi = sem("ln_hi")
        ln_scaled = sem("ln_scaled")
        ln_lo = sem("ln_lo")
        xn_hi = sem("xn_hi")
        xn_lo = sem("xn_lo")
        ffn_added = sem("ffn_added")
        parts_ready = sem("parts_ready")
        gathered = sem("gathered")
        stats_ready = sem("stats_ready")
        rstd_step = sem("rstd_step")
        rstd_ready = sem("rstd_ready")
        y_ready = sem("y_ready")
        biased = {part: sem(f"biased_{part}") for part in ("prev", "next")}
        res_ready = sem("res_ready")

        def quarter(w, i):
            return w.rearrange("(c p) n -> p c n", p=P)[:, :, i * SEQ:(i + 1) * SEQ]

        def heads_of(i):
            return wo.rearrange("(h d) n -> d h n", d=HD)[:, i * GROUP:(i + 1) * GROUP, :]

        def part_of(t, i):
            return [t[:, s, :, i * SEQ:(i + 1) * SEQ] for s in range(2)]

        def wo_part(i):
            return [wo_s[:, s, i * GROUP:(i + 1) * GROUP, :] for s in range(2)]

        stage_c = rope_cos[:, :, :]
        stage_s = rope_sin[:, :, :]
        stage_r = x_res[:, :, :].rearrange("p k e -> p (k e)").rearrange("p (c n) -> p c n", c=2)
        stage_rh = x_res[:, :, :]
        stage_p = probs[:, :, :, :].rearrange("p a k n -> p a (k n)")
        stage_ph = probs[:, :, :, :].rearrange("p a k n -> p (a k n)").rearrange("p (h n) -> p h n", h=GROUP)
        PIECES = [
            (stage_c, 0, quarter(wk, 0), part_of(wk_s, 0)),
            (stage_s, 1, quarter(wq, 0), part_of(wq_s, 0)),
            (stage_r, 2, quarter(wv, 0), part_of(wv_s, 0)),
            (stage_p, 3, quarter(wq, 1), part_of(wq_s, 1)),
            (stage_ph, 3, heads_of(0), wo_part(0)),
            (stage_r, 2, quarter(wq, 2), part_of(wq_s, 2)),
            (stage_rh, 2, heads_of(1), wo_part(1)),
            (stage_r, 2, quarter(wq, 3), part_of(wq_s, 3)),
            (stage_rh, 2, heads_of(2), wo_part(2)),
            (stage_rh, 2, heads_of(3), wo_part(3)),
        ]
        NEEDS = {"K": lambda i: 0, "V": lambda i: 2, "Q": lambda i: (1, 3, 5, 7)[i // GROUP]}
        WO_PIECE = (4, 6, 8, 9)

        def staged_before(n):
            return [i for i in range(n) if PIECES[i][1] == PIECES[n][1]]

        def passes(eng):
            yield Phase("prologue", -1)
            yield Phase("first", 0)
            with eng.Fori(1, BATCHES - 1) as b:
                yield Phase("middle", b)
            yield Phase("last", BATCHES - 1)
            yield Phase("epilogue", BATCHES)

        def bank_of(phase, x):
            return job_p[BANKED.parity(phase, x)]

        def roped(x, s):
            kind, i, _ = x
            return q_s[:, (i // GROUP) % 2, s, :, i % GROUP, :] if kind == "Q" else k_s[:, i % 2, s, :]

        def as_roped(x, ap):
            return ap.rearrange("p (c q) -> p c q", q=CHUNK) if x[0] == "Q" else ap

        def norm_of(x):
            if x[0].startswith("a"):
                return NORMS[2], x_mid
            return (NORMS[0], x_res) if x[2] == "prev" else (NORMS[1], x_in)

        def v_part(i, s):
            half, m = i
            width = NKV * HD // 2
            return v_s[:, s, 2 * m:2 * m + 2, half * width:(half + 1) * width]

        def xn_part(m, s):
            return xnT[:, s, :, 2 * P * m:2 * P * (m + 1)]

        block = ctx.enter_context(nc.Block())

        @block.sync
        def _(sp):
            def load_x(b):
                sp.dma_start(x_in[:, :, :], x_t[b]).then_inc(x_loaded, 16)

            def stage(n):
                where, s, src, _ = PIECES[n]
                if staged_before(n):
                    sp.wait_ge(split_lo, staged_before(n)[-1] + 1)
                sp.dma_start(where, src).then_inc(staged[s], 16)

            def stage_piece(_, x):
                stage(x[1])

            def load_next(phase, _):
                if phase.has("next"):
                    sp.wait_ge(ffn_added, FFN_OUT.start(phase))
                    load_x(phase.b + 1)

            def store_batch(phase, _):
                sp.wait_ge(ffn_added, FFN_OUT.after(phase, ("FO", 1, "prev")))
                sp.dma_start(out_t[phase.b - 1], x_res[:, :, :]).then_inc(out_stored, 16)

            def shift_values(phase, x):
                half = x[1]
                sp.wait_ge(v_lo, VALUES.after(phase, ("V", (half, 1), "cur" if half else "next")))
                cols = slice(half * NKV * HD // 2, (half + 1) * NKV * HD // 2)
                for s in range(2):
                    sp.dma_start(v_odd[0:CHUNK, s, :, cols].bitcast(F32),
                                 v_s[CHUNK:P, s, 0:BLOCKS - 1, cols].bitcast(F32)).then_inc(v_shifted, 16)
                    sp.dma_start(v_odd[CHUNK:P, s, :, cols].bitcast(F32),
                                 v_s[0:CHUNK, s, 1:BLOCKS, cols].bitcast(F32)).then_inc(v_shifted, 16)

            sp.dma_start(ln_full[:, :, :], ffn_wT.rearrange("(c p) n -> p c n", p=P)).then_inc(tern_in, 16)
            load_x(0)
            for dst, src in ((identf, ident), (gamma_s, gamma), (beta_s, beta), (half_b, ffn_b.partition_broadcast(P)),
                             (bo_t, bo.partition_broadcast(P))):
                sp.dma_start(dst[:, :], src).then_inc(rows_in, 16)
            for n in range(3):
                stage(n)
            for dst, src in ((bq_s, bq), (bk_s, bk), (bv_s, bv), (cos_t, cosT), (sin_t, sinT),
                             (identb, ident_bf), (mask_s, mask)):
                sp.dma_start(dst[:, :], src).then_inc(consts_in, 16)
            stage(3)
            for phase in passes(sp):
                for x in phase.steps(SYNC):
                    {"load": load_next, "stage": stage_piece, "shift": shift_values, "store": store_batch}[x[0]](phase, x)
            sp.wait_ge(out_stored, 16 * BATCHES)

        @block.tensor
        def _(pe):
            def three(dst, a, b, first, last, clears):
                for i, (p, q) in enumerate(((0, 0), (0, 1), (1, 0))):
                    mm = nc.tensor.matmul(dst, a(p), b(q), start=first and clears and i == 0,
                                          stop=last and i == 2, skip_group_check=True)
                return mm

            def scores(phase, x):
                u, (g, t) = phase.unit(x), divmod(x[1], BLOCKS)
                if t == 0:
                    pe.wait_ge(rope_lo, ROPED.after(phase, ("Q", GROUP * g + GROUP - 1, "cur")) if g
                               else ROPED.start(phase))
                if not (phase.name == "first" and x[1] < 2):
                    pe.wait_ge(exp_ready, u - 1)
                dst = scores_p[x[1] % 2]
                off = 0 if t == 0 else 2 * P
                nc.tensor.matmul(dst[:, :, :], identb[:, :], mask_s[:, off:off + 4 * P],
                                 start=True, stop=False, skip_group_check=True)
                for cc in range(2):
                    c = 2 * t + cc
                    w0 = CHUNK * max(c - 1, 0)
                    for pair in range(2):
                        mm = three(dst[:, 2 * cc + pair, :],
                                   lambda s: q_s[:, g % 2, s, c, 2 * pair:2 * pair + 2, :],
                                   lambda s: k_s[:, g % 2, s, w0:w0 + P], False, True, False)
                mm.then_inc(scores_ready, 1)

            def project(phase, x):
                u, (g, t) = phase.unit(x), divmod(x[1], BLOCKS)
                pe.wait_ge(heads_lo, u + 1)
                if phase.name == "first" and t == 0:
                    pe.wait_ge(split_lo, WO_PIECE[g] + 1)
                if x[1] == 0 and phase.has("prev"):
                    pe.wait_ge(attn_read, 2 * phase.b)
                for h in range(GROUP):
                    mm = three(attn_p[t // 2][:, t % 2, :], lambda s: headsT[:, s, h, :, :],
                               lambda s: wo_s[:, s, GROUP * g + h, :],
                               g == 0 and h == 0, g == NKV - 1 and h == GROUP - 1, t % 2 == 0)
                mm.then_inc(projected, 1)

            def values(phase, x):
                u, (g, t) = phase.unit(x), divmod(x[1], BLOCKS)
                pe.wait_ge(probsT_lo, u + 1)
                if x[1] in (0, UNITS // 2):
                    pe.wait_ge(v_shifted, 64 * (SHIFTS.after(phase, ("V", (1, 1), "cur")) if x[1]
                                                else SHIFTS.start(phase)))
                for cc in range(2):
                    c = 2 * t + cc
                    src, at = (v_s, max(c - 1, 0) // 2) if c == 0 or c % 2 else (v_odd, c // 2 - 1)
                    mm = three(heads_p[:, :, cc, :], lambda s: src[:, s, at, g * HD:(g + 1) * HD],
                               lambda s: probsT[:, s, cc, :], True, True, cc == 0)
                mm.then_inc(heads_ready, 1)

            def transpose_probs(phase, x):
                u = phase.unit(x)
                pe.wait_ge(probs_ready, u + 1)
                for k in range(4):
                    mm = nc.tensor.transpose(probsT_p[:, k, :], probs[:, x[1] % 2, k, :], identf[:, :])
                mm.then_inc(probsT_ready, 1)

            def wait_for_bank(phase, x):
                was, n = last_in_bank(phase, x)
                if was is None:
                    return
                if was[0] in ("Q", "K"):
                    pe.wait_ge(rope_cosed, n)
                elif was[0] == "V":
                    pe.wait_ge(v_lo, n)
                elif was[0] == "YT":
                    pe.wait_ge(ln_scaled, 2 * n)
                elif was[0] == "FO":
                    pe.wait_ge(ffn_added, n)
                elif was[0] == "XT":
                    pe.wait_ge(xn_lo, n)

            def job(phase, x):
                kind, i, _ = x
                bank = bank_of(phase, x)
                wait_for_bank(phase, x)
                if kind in NEEDS and phase.name in ("prologue", "first"):
                    pe.wait_ge(split_lo, NEEDS[kind](i) + 1)
                if x == ("K", 0, "next"):
                    pe.wait_ge(xn_lo, XN.after(phase, ("XT", 1, "next")))
                if kind in ("Q", "K"):
                    w = wq_s if kind == "Q" else wk_s
                    for e in range(EC):
                        mm = three(bank[:, :], lambda s: w[:, s, e, i * HD:(i + 1) * HD],
                                   lambda s: xnT[:, s, e, :], e == 0, e == EC - 1, True)
                if kind == "V":
                    half, m = i
                    width = NKV * HD // 2
                    for k in range(2):
                        at = (2 * m + k) * P
                        for e in range(EC):
                            mm = three(bank[:, k * width:(k + 1) * width], lambda s: xnT[:, s, e, at:at + P],
                                       lambda s: wv_s[:, s, e, half * width:(half + 1) * width],
                                       e == 0, e == EC - 1, k == 0)
                if kind in ("YT", "XT"):
                    pe.wait_ge(y_ready, Y_HALVES.after(phase, x))
                    for e in range(EC):
                        for k in range(2):
                            at = (2 * e + k) * P
                            mm = nc.tensor.transpose(bank[:, at:at + P], y[:, k, e * P:(e + 1) * P], identf[:, :])
                if kind == "FO":
                    pe.wait_ge(ln_lo, FFN_OUT.after(phase, x))
                    for k in range(2):
                        for e in range(EC):
                            for s in range(2):
                                mm = nc.tensor.matmul(bank[:, k * E:(k + 1) * E], lnT[:, s, e, k * P:(k + 1) * P],
                                                      w_tern[:, e, :], start=k == 0 and e == 0 and s == 0,
                                                      stop=e == EC - 1 and s == 1, skip_group_check=True)
                mm.then_inc(job_ready, 1)

            pe.wait_ge(abs_summed, 2)
            nc.tensor.matmul(scores_p[0][:, 0, 0:1], y[:, 0, 0:P], thr[:, 0:1],
                             start=True, stop=True).then_inc(scale_ready, 1)
            pe.wait_ge(rows_in, 16 * 5)
            pe.wait_ge(tern_ready, 1)
            for phase in passes(pe):
                if phase.name == "first":
                    pe.wait_ge(consts_in, 16 * 7)
                for x in phase.steps(TENSOR):
                    {"S": scores, "T": transpose_probs, "W": values, "O": project}.get(x[0], job)(phase, x)

        @block.vector
        def _(dve):
            def split_low(_, x):
                n = x[1]
                where, _, _, dst = PIECES[n]
                dve.wait_ge(split_hi, n + 1)
                nc.vector.tensor_tensor(dst[1], where, dst[0].bitcast(F32), ALU.subtract).then_inc(split_lo, 1)

            def max_of(phase, x):
                i = x[1] % 2
                dve.wait_ge(scores_ready, phase.unit(x) + 1)
                nc.vector.tensor_reduce(neg_max[:, i, :], scores_p[i][:, :, :], AX.X, ALU.max,
                                        negate=True).then_inc(max_ready, 1)

            def invert_sums(phase, x):
                i = x[1] % 2
                dve.wait_ge(exp_ready, phase.unit(x) + 1)
                nc.vector.reciprocal(inv_sum[:, i, :], row_sum[:, i, :]).then_inc(inv_ready, 1)

            def heads_low(phase, x):
                g = x[1] // BLOCKS
                dve.wait_ge(heads_hi, phase.unit(x) + 1)
                nc.vector.scalar_tensor_tensor(
                    out=headsT[:, 1, :, :, :].rearrange("p h c q -> p (h c q)"), in0=heads_p[:, :, :, :].rearrange("p h c q -> p (h c q)"),
                    scalar=bv_s[:, g:g + 1], in1=headsT[:, 0, :, :, :].rearrange("p h c q -> p (h c q)").bitcast(F32),
                    op0=ALU.add, op1=ALU.subtract).then_inc(heads_lo, 1)

            def probsT_low(phase, x):
                dve.wait_ge(probsT_hi, phase.unit(x) + 1)
                nc.vector.tensor_tensor(probsT[:, 1, :, :], probsT_p[:, :, :].rearrange("p (c a) n -> p c (a n)", c=2),
                                        probsT[:, 0, :, :].bitcast(F32), ALU.subtract).then_inc(probsT_lo, 1)

            def rope_end(phase, x):
                x = (x[0].removeprefix("end_"), *x[1:])
                dve.wait_ge(rope_hi, ROPED.after(phase, x))
                nc.vector.tensor_tensor(roped(x, 1), as_roped(x, rope_cos[:, ROPED.parity(phase, x), :]),
                                        roped(x, 0).bitcast(F32), ALU.subtract).then_inc(rope_lo, 1)

            def ffn_in_low(phase, x):
                x = ("YT", *x[1:])
                dve.wait_ge(ln_hi, FFN_IN.after(phase, x))
                nc.vector.tensor_tensor(lnT[:, 1, :, :], ln_full[:, :, :], lnT[:, 0, :, :].bitcast(F32),
                                        ALU.subtract).then_inc(ln_lo, 1)

            def take(phase, x):
                kind, i, part = x
                bank = bank_of(phase, x)
                halves = "p (k n) -> p k n"
                dve.wait_ge(job_ready, BANKED.after(phase, x))
                if kind in ("Q", "K"):
                    dve.wait_ge(rope_swapped, ROPED.after(phase, x))
                    n = ROPED.before(phase, x)
                    if not (phase.name == "prologue" and n < 2):
                        dve.wait_ge(rope_lo, n - 1)
                    r = ROPED.parity(phase, x)
                    if x == ("K", 0, "next") and phase.name == "prologue":
                        dve.wait_ge(consts_in, 16 * 7)
                    bias = (bq_s if kind == "Q" else bk_s)[:, i:i + 1]
                    nc.vector.scalar_tensor_tensor(
                        out=rope_cos[:, r, :], in0=bank[:, :], scalar=bias, in1=cos_t[:, :],
                        op0=ALU.add, op1=ALU.mult).then_inc(rope_cosed, 1)
                if kind == "V":
                    dve.wait_ge(v_hi, VALUES.after(phase, x))
                    nc.vector.tensor_tensor(v_part(i, 1), bank[:, :].rearrange(halves, k=2), v_part(i, 0).bitcast(F32),
                                            ALU.subtract).then_inc(v_lo, 1)
                if kind == "XT":
                    dve.wait_ge(xn_hi, XN.after(phase, x))
                    nc.vector.tensor_tensor(xn_part(i, 1), bank[:, :].rearrange(halves, k=2),
                                            xn_part(i, 0).bitcast(F32), ALU.subtract).then_inc(xn_lo, 1)
                if kind == "YT":
                    if not (phase.name == "prologue" and i == 0):
                        dve.wait_ge(ln_lo, FFN_IN.before(phase, x))
                    for e in range(EC):
                        nc.vector.tensor_scalar(ln_full[:, e, :], bank[:, e * 2 * P:(e + 1) * 2 * P],
                                                gamma_s[:, e:e + 1], beta_s[:, e:e + 1],
                                                ALU.mult, ALU.add).then_inc(ln_scaled, 1)
                if kind == "FO":
                    src, dst = (x_res, x_res) if part == "prev" else (x_in, x_mid)
                    dve.wait_ge(biased[part], BIASED[part].after(phase, ("YT", i, part)))
                    if part == "next" and phase.has("cur"):
                        dve.wait_ge(res_ready, phase.b + 1)
                    nc.vector.scalar_tensor_tensor(
                        out=dst[:, 2 * i:2 * i + 2, :], in0=bank[:, :].rearrange(halves, k=2), scalar=0.5,
                        in1=src[:, 2 * i:2 * i + 2, :], op0=ALU.mult, op1=ALU.add).then_inc(ffn_added, 1)

            def statistics(phase, x):
                norm, src = norm_of(x)
                blocks = range(BLOCKS)
                if x[0] == "astats":
                    blocks = blocks[2 * x[1]:2 * x[1] + 2]
                    dve.wait_ge(ffn_added, FFN_OUT.after(phase, ("FO", x[1], "next")))
                elif x[2] == "prev":
                    dve.wait_ge(attn_read, 2 * phase.b)
                else:
                    dve.wait_ge(x_loaded, 16 * (phase.b + 2))
                if not (phase.name == "prologue" and norm == NORMS[1]):
                    dve.wait_ge(stats_ready, NORMED.before(phase, norm))
                for k in blocks:
                    nc.vector.bn_stats(parts[:, k, :], src[:, k, :]).then_inc(parts_ready, 1)
                if x[0] == "stats" or x[1]:
                    gather_statistics(phase, norm)

            def gather_statistics(phase, norm):
                done = 5 * NORMED.before(phase, norm)
                dve.wait_ge(parts_ready, BLOCKS * NORMED.after(phase, norm))
                even, odd = parts[:, :, 0:3], parts[:, :, 3:6]
                nc.vector.tensor_tensor(sums[:, 0, :], even[:, :, 1], odd[:, :, 1], ALU.add).then_inc(gathered, 1)
                nc.vector.tensor_tensor(sums[:, 1, :], even[:, :, 1], odd[:, :, 1], ALU.subtract).then_inc(gathered, 1)
                nc.vector.tensor_tensor(sums[:, 2, :], even[:, :, 2], odd[:, :, 2], ALU.add).then_inc(gathered, 1)
                dve.wait_ge(gathered, done + 2)
                nc.vector.tensor_scalar(stats[:, :, 0], sums[:, 0, :], 0.5, None, ALU.mult).then_inc(gathered, 1)
                nc.vector.scalar_tensor_tensor(out=sums[:, 3, :], in0=sums[:, 1, :], scalar=0.25, in1=sums[:, 1, :],
                                               op0=ALU.mult, op1=ALU.mult).then_inc(gathered, 1)
                dve.wait_ge(gathered, done + 5)
                nc.vector.scalar_tensor_tensor(out=stats[:, :, 1], in0=sums[:, 2, :], scalar=1.0 / E,
                                               in1=sums[:, 3, :], op0=ALU.mult, op1=ALU.add).then_inc(stats_ready, 1)

            def normalize(phase, x):
                (norm, src), m = norm_of(x), x[1]
                dve.wait_ge(rstd_ready, NORMED.after(phase, norm))
                if x == ("anorm", 1, "next"):
                    dve.wait_ge(job_ready, BANKED.after(phase, ("XT", 0, "next")))
                for k in range(2):
                    at = 2 * m + k
                    ins = nc.vector.tensor_scalar(y[:, k, :], src[:, at, :], stats[:, at, 0:1], rstd[:, at:at + 1],
                                                  ALU.subtract, ALU.mult)
                ins.then_inc(y_ready, 1)

            def after_attention(phase, _):
                dve.wait_ge(projected, UNITS * phase.b)
                dve.wait_ge(res_ready, phase.b)
                for m in range(2):
                    nc.vector.tensor_tensor(x_res[:, 2 * m:2 * m + 2, :], attn_p[m][:, :, :],
                                            x_res[:, 2 * m:2 * m + 2, :], ALU.add).then_inc(attn_read, 1)

            nc.vector.memset(y[:, 0, 0:P], 1.0).then_inc(abs_summed, 1)
            dve.wait_ge(tern_in, 16)
            nc.vector.tensor_reduce(thr[:, 0:1], ln_full[:, :, :].rearrange("p c n -> p (c n)"), AX.X, ALU.add,
                                    apply_absolute_value=True).then_inc(abs_summed, 1)
            dve.wait_ge(scale_ready, 1)
            nc.vector.tensor_scalar(thr[:, 1:2], scores_p[0][:, 0, 0:1], 1.0 / (E * E), Q_EPS,
                                    ALU.mult, ALU.add).then_inc(thr_step, 1)
            dve.wait_ge(thr_step, 1)
            nc.vector.tensor_scalar(thr[:, 2:3], thr[:, 1:2], 0.5, None, ALU.mult).then_inc(thr_step, 1)
            dve.wait_ge(thr_step, 2)
            nc.vector.tensor_scalar(x_mid[:, 0:2, :], ln_full[:, :, :], thr[:, 2:3], None,
                                    ALU.is_gt).then_inc(thr_step, 1)
            nc.vector.tensor_scalar(x_mid[:, 2:4, :], ln_full[:, :, :], -1.0, thr[:, 2:3],
                                    ALU.mult, ALU.is_gt).then_inc(thr_step, 1)
            dve.wait_ge(thr_step, 4)
            nc.vector.tensor_tensor(w_tern[:, :, :], x_mid[:, 0:2, :], x_mid[:, 2:4, :],
                                    ALU.subtract).then_inc(tern_ready, 1)
            dve.wait_ge(rows_in, 16 * 5)
            for phase in passes(dve):
                for x in phase.steps(VECTOR):
                    {"max": max_of, "inv": invert_sums, "heads": heads_low, "probsT": probsT_low,
                     "end_Q": rope_end, "end_K": rope_end, "end_YT": ffn_in_low, "evac": after_attention, "w": split_low,
                     "stats": statistics, "astats": statistics, "norm": normalize,
                     "anorm": normalize}.get(x[0], take)(phase, x)

        @block.scalar
        def _(act):
            def split_high(_, x):
                n = x[1]
                where, s, _, dst = PIECES[n]
                act.wait_ge(staged[s], 16 * (len(staged_before(n)) + 1))
                nc.scalar.activation(dst[0], where, ACT.Copy).then_inc(split_hi, 1)

            def exp_of(phase, x):
                i = x[1] % 2
                act.wait_ge(max_ready, phase.unit(x) + 1)
                if phase.name == "first" and x[1] == 0:
                    act.wait_ge(split_lo, WO_PIECE[0] + 1)
                for k in range(4):
                    ins = nc.scalar.activation(probs[:, i, k, :], scores_p[i][:, k, :], ACT.Exp,
                                               bias=neg_max[:, i, k:k + 1], accum_out=row_sum[:, i, k:k + 1])
                ins.then_inc(exp_ready, 1)

            def heads_high(phase, x):
                g = x[1] // BLOCKS
                act.wait_ge(heads_ready, phase.unit(x) + 1)
                nc.scalar.activation(headsT[:, 0, :, :, :].rearrange("p h c q -> p (h c q)"), heads_p[:, :, :, :].rearrange("p h c q -> p (h c q)"),
                                     ACT.Identity, bias=bv_s[:, g:g + 1]).then_inc(heads_hi, 1)

            def probsT_high(phase, x):
                act.wait_ge(probsT_ready, phase.unit(x) + 1)
                nc.scalar.activation(probsT[:, 0, :, :], probsT_p[:, :, :].rearrange("p (c a) n -> p c (a n)", c=2),
                                     ACT.Copy).then_inc(probsT_hi, 1)

            def rope_end(phase, x):
                x = (x[0].removeprefix("end_"), *x[1:])
                kind, i, part = x
                act.wait_ge(rope_added, ROPED.after(phase, x))
                g = (i // GROUP if kind == "Q" else i) + (NKV if part == "next" else 0)
                if phase.has("cur") and not (phase.name == "first" and g == 1):
                    act.wait_ge(scores_ready, UNITS * phase.b + BLOCKS * (g - 1))
                nc.scalar.activation(roped(x, 0), as_roped(x, rope_cos[:, ROPED.parity(phase, x), :]),
                                     ACT.Copy).then_inc(rope_hi, 1)

            def take(phase, x):
                kind, i, part = x
                bank = bank_of(phase, x)
                halves = "p (k n) -> p k n"
                act.wait_ge(job_ready, BANKED.after(phase, x))
                if kind in ("Q", "K"):
                    r = ROPED.parity(phase, x)
                    bias = (bq_s if kind == "Q" else bk_s)[:, i:i + 1]
                    if x == ("K", 0, "next") and phase.name == "prologue":
                        act.wait_ge(consts_in, 16 * 7)
                        act.wait_ge(split_lo, 2)
                    n = ROPED.before(phase, x)
                    if not (phase.name == "prologue" and n < 2):
                        act.wait_ge(rope_added, n - 1)
                    nc.scalar.activation(rope_sin[0:HALF, r, :], bank[HALF:P, :], ACT.Identity, bias=bias[HALF:P, :])
                    nc.scalar.activation(rope_sin[HALF:P, r, :], bank[0:HALF, :], ACT.Identity,
                                         bias=bias[0:HALF, :]).then_inc(rope_swapped, 1)
                if kind == "V":
                    if i[0] == 1 and phase.has("prev"):
                        act.wait_ge(heads_ready, UNITS * phase.b)
                    if i[0] == 0 and phase.has("cur"):
                        act.wait_ge(heads_ready, UNITS * phase.b + UNITS // 2)
                    nc.scalar.activation(v_part(i, 0), bank[:, :].rearrange(halves, k=2), ACT.Copy).then_inc(v_hi, 1)
                if kind == "XT":
                    nc.scalar.activation(xn_part(i, 0), bank[:, :].rearrange(halves, k=2), ACT.Copy).then_inc(xn_hi, 1)
                if kind == "YT":
                    act.wait_ge(ln_scaled, 2 * FFN_IN.after(phase, x))
                    nc.scalar.activation(lnT[:, 0, :, :], ln_full[:, :, :], ACT.Copy).then_inc(ln_hi, 1)

            act.wait_ge(rows_in, 16 * 5)
            for phase in passes(act):
                for x in phase.steps(SCALAR):
                    {"exp": exp_of, "heads": heads_high, "probsT": probsT_high, "end_Q": rope_end,
                     "end_K": rope_end, "w": split_high}.get(x[0], take)(phase, x)

        @block.gpsimd
        def _(pool):
            def scale_of(phase, x):
                norm, _ = norm_of(x)
                done = NORM_STEPS.before(phase, norm)
                var = stats[:, :, 1]
                pool.wait_ge(stats_ready, NORMED.after(phase, norm))
                nc.gpsimd.tensor_tensor(tmp[:, 0, :], var, eps[:, :], ALU.add).then_inc(rstd_step, 1)
                pool.wait_ge(rstd_step, done + 1)
                if norm[0] == "norm_attn":
                    nc.gpsimd.tensor_tensor(rstd[:, :], tmp[:, 0, :], minus_half[:, :], ALU.pow).then_inc(rstd_ready, 1)
                    return
                nc.gpsimd.tensor_tensor(tmp[:, 1, :], tmp[:, 0, :], minus_half[:, :], ALU.pow).then_inc(rstd_step, 1)
                pool.wait_ge(rstd_step, done + 2)
                nc.gpsimd.tensor_tensor(tmp[:, 2, :], var, tmp[:, 1, :], ALU.mult).then_inc(rstd_step, 1)
                pool.wait_ge(rstd_step, done + 3)
                nc.gpsimd.tensor_tensor(tmp[:, 3, :], tmp[:, 2, :], tmp[:, 1, :], ALU.mult).then_inc(rstd_step, 1)
                pool.wait_ge(rstd_step, done + 4)
                nc.gpsimd.tensor_tensor(tmp[:, 4, :], tmp[:, 3, :], eps[:, :], ALU.add).then_inc(rstd_step, 1)
                pool.wait_ge(rstd_step, done + 5)
                nc.gpsimd.tensor_tensor(tmp[:, 2, :], tmp[:, 4, :], minus_half[:, :], ALU.pow).then_inc(rstd_step, 1)
                pool.wait_ge(rstd_step, done + 6)
                nc.gpsimd.tensor_tensor(rstd[:, :], tmp[:, 1, :], tmp[:, 2, :], ALU.mult).then_inc(rstd_ready, 1)

            def normalize_probs(phase, x):
                i = x[1] % 2
                pool.wait_ge(inv_ready, phase.unit(x) + 1)
                nc.gpsimd.tensor_tensor(probs[:, i, :, :], probs[:, i, :, :],
                                        inv_sum[:, i, :].unsqueeze(2).to_broadcast([P, 4, P]),
                                        ALU.mult).then_inc(probs_ready, 1)

            def rope(phase, x):
                r = ROPED.parity(phase, x)
                if phase.name == "prologue" and x[:2] == ("K", 0):
                    pool.wait_ge(consts_in, 16 * 7)
                pool.wait_ge(rope_swapped, ROPED.after(phase, x))
                nc.gpsimd.tensor_tensor(rope_sin[:, r, :], rope_sin[:, r, :], sin_t[:, :], ALU.mult).then_inc(rope_sined, 1)
                pool.wait_ge(rope_sined, ROPED.after(phase, x))
                pool.wait_ge(rope_cosed, ROPED.after(phase, x))
                nc.gpsimd.tensor_tensor(rope_cos[:, r, :], rope_cos[:, r, :], rope_sin[:, r, :], ALU.add).then_inc(rope_added, 1)

            def bias_residual(phase, x):
                _, m, part = x
                buf = x_res if part == "prev" else x_in
                pool.wait_ge(y_ready, Y_HALVES.after(phase, ("YT", m, part)))
                nc.gpsimd.tensor_tensor(buf[:, 2 * m:2 * m + 2, :], buf[:, 2 * m:2 * m + 2, :],
                                        half_b[:, :].unsqueeze(1).to_broadcast([P, 2, E]), ALU.add).then_inc(biased[part], 1)

            def residual(phase, _):
                if phase.has("prev"):
                    pool.wait_ge(out_stored, 16 * phase.b)
                else:
                    pool.wait_ge(split_lo, len(PIECES))
                    pool.wait_ge(ffn_added, FFN_OUT.start(phase))
                nc.gpsimd.tensor_tensor(x_res[:, :, :], x_mid[:, :, :],
                                        bo_t[:, :].unsqueeze(1).to_broadcast([P, BLOCKS, E]), ALU.add).then_inc(res_ready, 1)

            nc.gpsimd.memset(minus_half[:, :], -0.5).then_inc(power_ready, 1)
            nc.gpsimd.memset(eps[:, :], LN_EPS).then_inc(power_ready, 1)
            pool.wait_ge(power_ready, 2)
            pool.wait_ge(rows_in, 16 * 5)
            nc.gpsimd.tensor_scalar(half_b[:, :], half_b[:, :], 0.5, None, ALU.mult).then_inc(bias_ready, 1)
            pool.wait_ge(bias_ready, 1)
            for phase in passes(pool):
                if phase.name == "prologue":
                    pool.wait_ge(x_loaded, 16)
                for x in phase.steps(GPSIMD):
                    {"probs": normalize_probs, "scale": scale_of, "ascale": scale_of, "bias": bias_residual,
                     "residual": residual}.get(x[0], rope)(phase, x)


def constants():
    half = np.arange(HALF, dtype=np.float32)
    freqs = np.float32(1.0) / np.float32(ROPE_BASE) ** (np.float32(2.0) * half / np.float32(HD))
    angles = (np.arange(SEQ, dtype=np.float32)[:, None] * freqs[None, :]).astype(np.float32).T.astype(np.float64)
    scale = float(HD) ** -0.25
    cosT = (np.concatenate([np.cos(angles)] * 2) * scale).astype(np.float32)
    sinT = (np.concatenate([-np.sin(angles), np.sin(angles)]) * scale).astype(np.float32)
    q = np.arange(P)[:, None] % CHUNK
    key = np.arange(P)[None, :]
    windowed = (key - CHUNK <= q) & (q - (key - CHUNK) <= WINDOW)
    causal = key <= q
    mask = np.concatenate([causal] * 2 + [windowed] * 4, axis=1)
    return cosT, sinT, np.where(mask, 0.0, MASKED), np.eye(P)


def kernel(L0_attn_x, L0_attn_Wq, L0_attn_bq, L0_attn_Wk, L0_attn_bk, L0_attn_Wv, L0_attn_bv, L0_attn_Wo,
           L0_attn_bo, L0_ffn_weight, L0_ffn_bias, L0_ffn_ln_gamma, L0_ffn_ln_beta):
    import ml_dtypes
    import concourse.bacc as bacc
    from concourse.bass_utils import run_bass_kernel_spmd

    def evens_first(w):
        w = np.asarray(w)
        heads = w.reshape(*w.shape[:-1], -1, HALF, 2)
        return np.ascontiguousarray(np.swapaxes(heads, -1, -2).reshape(w.shape))

    def by_head(b):
        return np.ascontiguousarray(np.asarray(b).reshape(-1, HD).T)

    cosT, sinT, mask, eye = constants()
    arrays = {
        "x": np.ascontiguousarray(L0_attn_x),
        "wq": evens_first(L0_attn_Wq), "bq": by_head(evens_first(L0_attn_bq)),
        "wk": evens_first(L0_attn_Wk), "bk": by_head(evens_first(L0_attn_bk)),
        "wv": np.ascontiguousarray(L0_attn_Wv), "bv": by_head(L0_attn_bv),
        "wo": np.ascontiguousarray(L0_attn_Wo), "bo": np.ascontiguousarray(L0_attn_bo),
        "ffn_wT": np.ascontiguousarray(np.asarray(L0_ffn_weight).T), "ffn_b": np.ascontiguousarray(L0_ffn_bias),
        "gamma": by_head(L0_ffn_ln_gamma), "beta": by_head(L0_ffn_ln_beta),
        "cosT": cosT, "sinT": sinT, "mask": mask.astype(ml_dtypes.bfloat16),
        "ident_bf": eye.astype(ml_dtypes.bfloat16), "ident": eye.astype(np.float32),
    }
    nc = bacc.Bacc("TRN2", target_bir_lowering=False, num_devices=1)
    args = [nc.dram_tensor(name, a.shape, mybir.dt.from_np(a.dtype), kind="ExternalInput").ap()
            for name, a in arrays.items()]
    out = nc.dram_tensor("out", (BATCHES, SEQ, E), F32, kind="ExternalOutput").ap()
    block_kernel(nc, *args, out)
    r = run_bass_kernel_spmd(nc, [arrays], core_ids=[0])
    return r.results[0]["out"]
```

```python
from contextlib import ExitStack

import numpy as np

import concourse.bass as bass
from concourse import mybir

F32 = mybir.dt.float32
F32R = mybir.dt.float32r
BF16 = mybir.dt.bfloat16
ALU = mybir.AluOpType
ACT = mybir.ActivationFunctionType
AX = mybir.AxisListType

P = 128
BATCHES, SEQ, E = 8, 512, 256
NQ, NKV, HD = 16, 4, 128
WINDOW = 64
ROPE_BASE = 10000.0
LN_EPS = 1e-5
Q_EPS = 1e-5
MASKED = -1e30

GROUP = NQ // NKV
CHUNK = WINDOW
BLOCKS = SEQ // P
EC = E // P
UNITS = NKV * BLOCKS
HALF = HD // 2
COLUMNS = (NQ, NKV, NKV, EC, EC)

TENSOR = """
    K1c Q4c
    S0c O13p W14p T15p
    S1c Q5c V10c O14p W15p T0c Q6c
    S2c Q7c O15p W0c YT0p T1c
    S3c K2c Q8c O0c W1c T2c Q9c
    S4c O1c W2c V11c T3c
    S5c FO0p YT1p O2c W3c Q10c T4c Q11c
    S6c O3c W4c T5c FO1p K3c
    S7c YT0n O4c W5c T6c Q12c
    S8c O5c FO0n W6c YT1n T7c Q13c
    S9c Q14c O6c W7c FO1n T8c
    S10c Q15c XT0n O7c W8c T9c
    S11c XT1n O8c W9c T10c K0n
    S12c Q0n O9c W10c T11c
    S13c Q1n V00n O10c W11c T12c
    S14c Q2n O11c W12c T13c Q3n
    S15c V01n O12c W13c T14c
"""
VECTOR = """
    heads13p probsT14p K1c evac0p
    max0c Q4c
    max1c heads14p inv0c end_K1c probsT15p Q5c w8f stats0p inv1c V10c probsT0c heads15p end_Q4c norm0p Q6c end_Q5c
    max2c evac1p Q7c YT0p heads0c stats1p inv2c probsT1c end_Q6c K2c end_Q7c
    max3c Q8c heads1c probsT2c stats0n inv3c
    max4c end_K2c end_YT0p Q9c tern0i norm1p heads2c V11c probsT3c tern1i
    max5c inv4c FO0p YT1p norm0n stats1n end_Q8c inv5c heads3c end_Q9c probsT4c end_YT1p
    max6c Q10c Q11c w9f inv6c FO1p heads4c probsT5c end_Q10c
    max7c K3c end_Q11c YT0n inv7c heads5c probsT6c norm1n end_YT0n w0i
    max8c Q12c end_K3c FO0n YT1n heads6c inv8c astats0n probsT7c end_YT1n w1i
    max9c Q13c end_Q12c anorm0n Q14c FO1n heads7c inv9c astats1n probsT8c
    max10c w2i end_Q13c anorm1n Q15c inv10c heads8c
    max11c w3i w4i probsT9c XT0n XT1n w5i w6i end_Q14c end_Q15c w7i heads9c inv11c
    max12c probsT10c K0n add_K0i Q0n inv12c end_K0n heads10c
    max13c probsT11c Q1n inv13c heads11c add_Q0i
    max14c probsT12c V00n add_Q1i end_Q0n Q2n inv14c heads12c end_Q1n probsT13c Q3n
    max15c add_Q2i add_Q3i V01n end_Q2n end_Q3n inv15c
"""
SCALAR = """
    heads13p probsT14p K1c Q4c heads14p probsT15p w8f
    exp0c end_K1c Q5c mask2c
    exp1c V10c probsT0c heads15p end_Q4c Q6c mask3c end_Q5c Q7c heads0c probsT1c
    exp2c end_Q6c K2c end_Q7c Q8c mask4c heads1c probsT2c YT0p
    exp3c end_K2c Q9c mask5c heads2c w9f w0i V11c probsT3c
    exp4c end_Q8c mask6c
    exp5c YT1p heads3c end_Q9c mask7c probsT4c Q10c Q11c
    exp6c heads4c probsT5c end_Q10c mask8c K3c end_Q11c
    exp7c w1i heads5c probsT6c mask9c YT0n end_K3c Q12c
    exp8c heads6c mask10c probsT7c YT1n Q13c end_Q12c w2i Q14c
    exp9c heads7c probsT8c end_Q13c mask11c Q15c
    exp10c heads8c end_Q14c probsT9c XT0n w3i w4i XT1n w5i w6i mask12c w7i end_Q15c
    exp11c heads9c probsT10c mask13c K0n Q0n
    exp12c heads10c end_K0n probsT11c mask14c Q1n V00n
    exp13c heads11c end_Q0n mask15c probsT12c Q2n
    exp14c heads12c end_Q1n probsT13c Q3n mask0n V01n end_Q2n
    exp15c end_Q3n mask1n
"""
GPSIMD = """
    K1c Q4c
    probs0c Q5c scale0p
    probs1c Q6c Q7c
    probs2c K2c scale1p Q8c
    probs3c bias0p Q9c scale0n
    probs4c scale1n bias1p half0i
    probs5c Q10c Q11c
    probs6c K3c residual0c bias0n
    probs7c Q12c bias1n
    probs8c ascale0n Q13c Q14c
    probs9c ascale1n Q15c
    probs10c
    probs11c K0n
    probs12c Q0n
    probs13c Q1n Q2n
    probs14c Q3n
    probs15c
"""

SYNC = """
    load0c stage8i stage9f store0p store1p shift1c shift0n
"""


def steps(table):
    found = []
    for step in table.split():
        name = step[:-1].rstrip("0123456789")
        index = step[len(name):-1]
        found.append((name, (int(index[0]), int(index[1])) if name == "V" else int(index or 0), PART[step[-1]]))
    return found


PART = {"p": "prev", "c": "cur", "n": "next", "i": "prologue", "f": "first"}
JOB_KINDS = ("K", "Q", "V", "YT", "FO", "XT")


class Phase:

    def __init__(self, name, b):
        self.name, self.b, self.parts = name, b, PARTS[name]

    def has(self, part):
        return part in self.parts

    def steps(self, table):
        return [x for x in steps(table) if x[2] in (*self.parts, self.name)]

    def unit(self, x):
        return UNITS * (self.b + {"prev": -1, "cur": 0, "next": 1}[x[2]]) + x[1]


PARTS = {
    "prologue": ("next",),
    "first": ("cur", "next"),
    "middle": ("prev", "cur", "next"),
    "last": ("prev", "cur"),
    "epilogue": ("prev",),
}
ORDER = list(PARTS)
MIDDLES = BATCHES - 2
ALL_JOBS = [x for x in steps(TENSOR) if x[0] in JOB_KINDS]
NORMS = [("norm2", 0, "prev"), ("norm2", 1, "prev"), ("norm1", 0, "next"), ("norm1", 1, "next"),
         ("norm_attn", 0, "next"), ("norm_attn", 1, "next")]


class Tally:

    def __init__(self, items, weight):
        self.items, self.weight = items, weight

    def in_pass(self, name):
        return sum(self.weight(x) for x in self.items if x[2] in PARTS[name])

    def start(self, phase):
        n = sum(self.in_pass(name) * (MIDDLES if name == "middle" else 1)
                for name in ORDER[:ORDER.index(phase.name)])
        return n + (phase.b - 1) * self.in_pass("middle") if phase.name == "middle" else n

    def before(self, phase, item):
        held = [x for x in self.items if x[2] in phase.parts]
        return self.start(phase) + sum(self.weight(x) for x in held[:held.index(item)])

    def after(self, phase, item):
        return self.before(phase, item) + self.weight(item)

    def parity(self, phase, item):
        assert self.in_pass("middle") % 2 == 0
        return self.before(Phase(phase.name, 1), item) % 2


def of(*kinds):
    return lambda x: int(x[0] in kinds)


BANKED = Tally(ALL_JOBS, lambda x: 1)
BY_KIND = {kind: Tally(ALL_JOBS, of(kind)) for kind in ("V", "YT", "FO", "XT")}
ROPED = Tally(ALL_JOBS, of("Q", "K"))
VALUES = BY_KIND["V"]
FFN_IN = BY_KIND["YT"]
FFN_OUT = BY_KIND["FO"]
XN = BY_KIND["XT"]
Y_HALVES = Tally(ALL_JOBS, of("YT", "XT"))
SHIFTS = Tally(ALL_JOBS, lambda x: int(x[0] == "V" and x[1][1] == 1))
BIASED = {part: Tally(ALL_JOBS, lambda x, part=part: int(x[0] == "YT" and x[2] == part)) for part in ("prev", "next")}
NORMED = Tally(NORMS, lambda x: 1)

def last_in_bank(phase, x):
    earlier = {"first": "prologue", "middle": "first", "last": "first", "epilogue": "last"}
    held = [y for y in ALL_JOBS if y[2] in phase.parts]
    if phase.name in earlier:
        held = [y for y in ALL_JOBS if y[2] in PARTS[earlier[phase.name]]] + held
    at = len(held) - 1 - held[::-1].index(x)
    if at < 2:
        return None, None
    was, between = held[at - 2], held[at - 1]
    tally = ROPED if was[0] in ("Q", "K") else BY_KIND[was[0]]
    return was, tally.before(phase, x) - tally.weight(between)


def block_kernel(nc, x, wq, wk, wv, wo, ffn_wT, columns, rows, rope_tables, mask, ident, out):
    x_t = x.rearrange("b (k p) e -> b p k e", p=P)
    out_t = out.rearrange("b (k p) e -> b p k e", p=P)

    with ExitStack() as ctx:
        def sb(name, shape, dt=F32):
            return ctx.enter_context(nc.sbuf_tensor(name, shape, dt))

        def psum(name, shape, dt=F32):
            return ctx.enter_context(nc.psum_tensor(name, shape, dt))

        def sem(name):
            return ctx.enter_context(nc.semaphore(name))

        wq_s = sb("wq_s", [P, 2, EC, NQ * HD], F32R)
        wk_s = sb("wk_s", [P, 2, EC, NKV * HD], F32R)
        wv_s = sb("wv_s", [P, 2, EC, NKV * HD], F32R)
        wo_s = sb("wo_s", [P, 2, NQ, E], F32R)
        w_tern = sb("w_tern", [P, EC, E], F32R)
        xnT = sb("xnT", [P, 2, EC, SEQ], F32R)
        lnT = sb("lnT", [P, 2, EC, 2 * P], F32R)
        ln_full = sb("ln_full", [P, EC, 2 * P])
        with nc.sbuf_tensor("staging_q", [P, 4, 2 * SEQ], F32) as staging_q:
            pass
        q_s = [sb(f"q_s{i}", [P, 2, SEQ // CHUNK, GROUP, CHUNK], F32R) for i in (1, 0)][::-1]
        k_s = sb("k_s", [P, 2, 2, SEQ], F32R)
        v_s = sb("v_s", [P, 2, BLOCKS, NKV * HD], F32R)
        v_odd = sb("v_odd", [P, 2, BLOCKS - 1, NKV * HD], F32R)
        probs = sb("probs", [P, 2, 4, P])
        probsT = sb("probsT", [P, 2, 2, GROUP * CHUNK], F32R)
        headsT = sb("headsT", [P, 2, GROUP, 2, CHUNK], F32R)
        neg_max = sb("neg_max", [P, 2, 4])
        row_sum = sb("row_sum", [P, 2, 4])
        inv_sum = sb("inv_sum", [P, 2, 4])
        rope_cos = sb("rope_cos", [P, 2, SEQ])
        rope_sin = sb("rope_sin", [P, 2, SEQ])
        rope_t = sb("rope_t", [P, 2, SEQ])
        cos_t, sin_t = rope_t[:, 0, :], rope_t[:, 1, :]
        x_in = sb("x_in", [P, BLOCKS, E])
        x_mid = sb("x_mid", [P, BLOCKS, E])
        x_res = sb("x_res", [P, BLOCKS, E])
        y = sb("y", [P, 2, E])
        rows_s = sb("rows_s", [P, 2, E])
        half_b, bo_t = rows_s[:, 0, :], rows_s[:, 1, :]
        mask_s = sb("mask_s", [P, 6 * P], BF16)
        identf = sb("identf", [P, P])
        columns_s = sb("columns_s", [P, sum(COLUMNS)])
        bq_s, bk_s, bv_s, gamma_s, beta_s = (columns_s[:, sum(COLUMNS[:i]):sum(COLUMNS[:i + 1])]
                                             for i in range(len(COLUMNS)))
        parts = sb("parts", [P, BLOCKS, 6])
        stats = sb("stats", [P, BLOCKS, 2])
        sums = sb("sums", [P, 4, BLOCKS])
        tmp = sb("tmp", [P, BLOCKS])
        rstd = sb("rstd", [P, BLOCKS])
        minus_half = sb("minus_half", [P, BLOCKS])
        eps = sb("eps", [P, BLOCKS])
        eps_twice = sb("eps_twice", [P, BLOCKS])
        thr = sb("thr", [P, 4])

        scores_p = [psum(f"scores_p{i}", [P, 4, P]) for i in range(2)]
        probsT_p = psum("probsT_p", [P, 4, P])
        heads_p = psum("heads_p", [P, GROUP, 2, CHUNK])
        job_p = [psum(f"job_p{i}", [P, SEQ]) for i in range(2)]
        attn_p = [psum(f"attn_p{i}", [P, 2, E]) for i in range(2)]

        consts_in = sem("consts_in")
        tern_in = sem("tern_in")
        rows_in = sem("rows_in")
        x_loaded = [sem(f"x_loaded{m}") for m in range(2)]
        out_stored = sem("out_stored")
        staged = [sem(f"staged{i}") for i in range(8)]
        split_hi = sem("split_hi")
        split_lo = sem("split_lo")
        v_shifted = sem("v_shifted")
        abs_summed = sem("abs_summed")
        scale_ready = sem("scale_ready")
        thr_step = sem("thr_step")
        tern_ready = sem("tern_ready")
        bias_ready = sem("bias_ready")
        power_ready = sem("power_ready")

        banks_open = sem("banks_open")
        mask_ready = sem("mask_ready")
        scores_ready = sem("scores_ready")
        max_ready = sem("max_ready")
        exp_ready = sem("exp_ready")
        inv_ready = sem("inv_ready")
        probs_ready = sem("probs_ready")
        probsT_ready = sem("probsT_ready")
        probsT_hi = sem("probsT_hi")
        probsT_lo = sem("probsT_lo")
        heads_ready = sem("heads_ready")
        heads_hi = sem("heads_hi")
        heads_lo = sem("heads_lo")
        projected = sem("projected")
        attn_read = sem("attn_read")

        job_ready = sem("job_ready")
        rope_swapped = sem("rope_swapped")
        rope_cosed = sem("rope_cosed")
        rope_sined = sem("rope_sined")
        rope_added = sem("rope_added")
        rope_hi = sem("rope_hi")
        rope_lo = sem("rope_lo")
        v_hi = sem("v_hi")
        v_lo = sem("v_lo")
        ln_hi = sem("ln_hi")
        ln_scaled = sem("ln_scaled")
        ln_lo = sem("ln_lo")
        xn_hi = sem("xn_hi")
        xn_lo = sem("xn_lo")
        ffn_added = sem("ffn_added")
        parts_ready = sem("parts_ready")
        gathered = sem("gathered")
        stats_ready = sem("stats_ready")
        rstd_step = sem("rstd_step")
        rstd_ready = sem("rstd_ready")
        y_ready = sem("y_ready")
        biased = {part: sem(f"biased_{part}") for part in ("prev", "next")}
        res_ready = sem("res_ready")

        def quarter(w, i):
            return w.rearrange("(c p) n -> p c n", p=P)[:, :, i * SEQ:(i + 1) * SEQ]

        def heads_of(i):
            return wo.rearrange("(h d) n -> d h n", d=HD)[:, i * GROUP:(i + 1) * GROUP, :]

        def part_of(t, i):
            return [t[:, s, :, i * SEQ:(i + 1) * SEQ] for s in range(2)]

        def wo_part(i):
            return [wo_s[:, s, i * GROUP:(i + 1) * GROUP, :] for s in range(2)]

        def as_heads(t):
            return t.rearrange("p c n -> p (c n)").rearrange("p (h n) -> p h n", h=GROUP)

        stage_r = x_res[:, :, :].rearrange("p k e -> p (k e)").rearrange("p (c n) -> p c n", c=2)
        stage_p = probs[:, :, :, :].rearrange("p a k n -> p a (k n)")
        stage_q = [staging_q[:, i, :].rearrange("p (c n) -> p c n", c=2) for i in range(4)]
        PIECES = [
            (rope_cos[:, :, :], 0, quarter(wk, 0), part_of(wk_s, 0)),
            (rope_sin[:, :, :], 1, quarter(wq, 0), part_of(wq_s, 0)),
            (stage_r, 2, quarter(wv, 0), part_of(wv_s, 0)),
            (stage_p, 3, quarter(wq, 1), part_of(wq_s, 1)),
            (as_heads(stage_q[0]), 4, heads_of(0), wo_part(0)),
            (stage_q[1], 5, quarter(wq, 2), part_of(wq_s, 2)),
            (as_heads(stage_q[2]), 6, heads_of(1), wo_part(1)),
            (stage_q[3], 7, quarter(wq, 3), part_of(wq_s, 3)),
            (as_heads(stage_r), 2, heads_of(2), wo_part(2)),
            (as_heads(stage_r), 2, heads_of(3), wo_part(3)),
        ]
        NEEDS = {"K": lambda i: 0, "V": lambda i: 2, "Q": lambda i: (1, 3, 5, 7)[i // GROUP]}
        WO_PIECE = (4, 6, 8, 9)

        def staged_before(n):
            return [i for i in range(n) if PIECES[i][1] == PIECES[n][1]]

        def passes(eng):
            yield Phase("prologue", -1)
            yield Phase("first", 0)
            with eng.Fori(1, BATCHES - 1) as b:
                yield Phase("middle", b)
            yield Phase("last", BATCHES - 1)
            yield Phase("epilogue", BATCHES)

        def bank_of(phase, x):
            return job_p[BANKED.parity(phase, x)]

        def roped(x, s):
            kind, i, _ = x
            return q_s[(i // GROUP) % 2][:, s, :, i % GROUP, :] if kind == "Q" else k_s[:, i % 2, s, :]

        def as_roped(x, ap):
            return ap.rearrange("p (c q) -> p c q", q=CHUNK) if x[0] == "Q" else ap

        def norm_of(x):
            if x[0].startswith("a"):
                return ("norm_attn", *x[1:]), x_mid
            return (("norm2", *x[1:]), x_res) if x[2] == "prev" else (("norm1", *x[1:]), x_in)

        def variance_factor(norm):
            return 1.0 if norm[0] == "norm_attn" else 1.0 + LN_EPS

        def v_part(i, s):
            half, m = i
            width = NKV * HD // 2
            return v_s[:, s, 2 * m:2 * m + 2, half * width:(half + 1) * width]

        def flat_heads(ap):
            return ap.rearrange("p h c q -> p (h c q)")

        def xn_part(m, s):
            return xnT[:, s, :, 2 * P * m:2 * P * (m + 1)]

        block = ctx.enter_context(nc.Block())

        @block.sync
        def _(sp):
            def load_x(b, m):
                sp.dma_start(x_in[:, 2 * m:2 * m + 2, :], x_t[b][:, 2 * m:2 * m + 2, :]).then_inc(x_loaded[m], 16)

            def stage(n):
                where, s, src, _ = PIECES[n]
                if staged_before(n):
                    sp.wait_ge(split_lo, staged_before(n)[-1] + 1)
                sp.dma_start(where, src).then_inc(staged[s], 16)

            def stage_piece(_, x):
                stage(x[1])

            def load_next(phase, _):
                if phase.has("next"):
                    sp.wait_ge(ffn_added, FFN_OUT.start(phase))
                    for m in range(2):
                        load_x(phase.b + 1, m)

            def store_half(phase, x):
                m = x[1]
                sp.wait_ge(ffn_added, FFN_OUT.after(phase, ("FO", m, "prev")))
                sp.dma_start(out_t[phase.b - 1][:, 2 * m:2 * m + 2, :], x_res[:, 2 * m:2 * m + 2, :]).then_inc(out_stored, 16)

            def shift_values(phase, x):
                half = x[1]
                sp.wait_ge(v_lo, VALUES.after(phase, ("V", (half, 1), "cur" if half else "next")))
                cols = slice(half * NKV * HD // 2, (half + 1) * NKV * HD // 2)
                for s in range(2):
                    sp.dma_start(v_odd[0:CHUNK, s, :, cols].bitcast(F32),
                                 v_s[CHUNK:P, s, 0:BLOCKS - 1, cols].bitcast(F32)).then_inc(v_shifted, 16)
                    sp.dma_start(v_odd[CHUNK:P, s, :, cols].bitcast(F32),
                                 v_s[0:CHUNK, s, 1:BLOCKS, cols].bitcast(F32)).then_inc(v_shifted, 16)

            load_x(0, 0)
            sp.dma_start(ln_full[:, :, :], ffn_wT.rearrange("(c p) n -> p c n", p=P)).then_inc(tern_in, 16)
            load_x(0, 1)
            for dst, src in ((identf[:, :], ident), (columns_s[:, :], columns), (rows_s[:, :, :], rows.partition_broadcast(P))):
                sp.dma_start(dst, src).then_inc(rows_in, 16)
            for n in range(3):
                stage(n)
            for dst, src in ((rope_t[:, :, :], rope_tables), (mask_s[:, :], mask)):
                sp.dma_start(dst, src).then_inc(consts_in, 16)
            for n in range(3, 8):
                stage(n)
            for phase in passes(sp):
                for x in phase.steps(SYNC):
                    {"load": load_next, "stage": stage_piece, "shift": shift_values, "store": store_half}[x[0]](phase, x)
            sp.wait_ge(out_stored, 2 * 16 * BATCHES)

        @block.tensor
        def _(pe):
            def three(dst, a, b, first, last, clears):
                for i, (p, q) in enumerate(((0, 0), (0, 1), (1, 0))):
                    mm = nc.tensor.matmul(dst, a(p), b(q), start=first and clears and i == 0,
                                          stop=last and i == 2, skip_group_check=True)
                return mm

            def scores(phase, x):
                u, (g, t) = phase.unit(x), divmod(x[1], BLOCKS)
                if t == 0:
                    pe.wait_ge(rope_lo, ROPED.after(phase, ("Q", GROUP * g + GROUP - 1, "cur")) if g
                               else ROPED.start(phase))
                pe.wait_ge(mask_ready, u + 1)
                dst = scores_p[x[1] % 2]
                for cc in range(2):
                    c = 2 * t + cc
                    w0 = CHUNK * max(c - 1, 0)
                    for pair in range(2):
                        mm = three(dst[:, 2 * cc + pair, :],
                                   lambda s: q_s[g % 2][:, s, c, 2 * pair:2 * pair + 2, :],
                                   lambda s: k_s[:, g % 2, s, w0:w0 + P], False, True, False)
                mm.then_inc(scores_ready, 1)

            def project(phase, x):
                u, (g, t) = phase.unit(x), divmod(x[1], BLOCKS)
                pe.wait_ge(heads_lo, u + 1)
                if phase.name == "first" and t == 0:
                    pe.wait_ge(split_lo, WO_PIECE[g] + 1)
                if g == 0 and t in (0, 2) and phase.has("prev"):
                    pe.wait_ge(attn_read, 2 * phase.b - (t == 0))
                for h in range(GROUP):
                    mm = three(attn_p[t // 2][:, t % 2, :], lambda s: headsT[:, s, h, :, :],
                               lambda s: wo_s[:, s, GROUP * g + h, :],
                               g == 0 and h == 0, g == NKV - 1 and h == GROUP - 1, t % 2 == 0)
                mm.then_inc(projected, 1)

            def values(phase, x):
                u, (g, t) = phase.unit(x), divmod(x[1], BLOCKS)
                pe.wait_ge(probsT_lo, u + 1)
                if x[1] in (0, UNITS // 2):
                    pe.wait_ge(v_shifted, 64 * (SHIFTS.after(phase, ("V", (1, 1), "cur")) if x[1]
                                                else SHIFTS.start(phase)))
                for cc in range(2):
                    c = 2 * t + cc
                    src, at = (v_s, max(c - 1, 0) // 2) if c == 0 or c % 2 else (v_odd, c // 2 - 1)
                    mm = three(heads_p[:, :, cc, :], lambda s: src[:, s, at, g * HD:(g + 1) * HD],
                               lambda s: probsT[:, s, cc, :], True, True, cc == 0)
                mm.then_inc(heads_ready, 1)

            def transpose_probs(phase, x):
                u = phase.unit(x)
                pe.wait_ge(probs_ready, u + 1)
                for k in range(4):
                    mm = nc.tensor.transpose(probsT_p[:, k, :], probs[:, x[1] % 2, k, :], identf[:, :])
                mm.then_inc(probsT_ready, 1)

            def wait_for_bank(phase, x):
                was, n = last_in_bank(phase, x)
                if was is None:
                    return
                if was[0] in ("Q", "K"):
                    pe.wait_ge(rope_cosed, n)
                elif was[0] == "V":
                    pe.wait_ge(v_lo, n)
                elif was[0] == "YT":
                    pe.wait_ge(ln_scaled, 2 * n)
                elif was[0] == "FO":
                    pe.wait_ge(ffn_added, n)
                elif was[0] == "XT":
                    pe.wait_ge(xn_lo, n)

            def job(phase, x):
                kind, i, _ = x
                bank = bank_of(phase, x)
                wait_for_bank(phase, x)
                if kind in NEEDS and phase.name in ("prologue", "first"):
                    pe.wait_ge(split_lo, NEEDS[kind](i) + 1)
                if x == ("K", 0, "next"):
                    pe.wait_ge(xn_lo, XN.after(phase, ("XT", 1, "next")))
                if kind in ("Q", "K"):
                    w = wq_s if kind == "Q" else wk_s
                    for e in range(EC):
                        mm = three(bank[:, :], lambda s: w[:, s, e, i * HD:(i + 1) * HD],
                                   lambda s: xnT[:, s, e, :], e == 0, e == EC - 1, True)
                if kind == "V":
                    half, m = i
                    width = NKV * HD // 2
                    for k in range(2):
                        at = (2 * m + k) * P
                        for e in range(EC):
                            mm = three(bank[:, k * width:(k + 1) * width], lambda s: xnT[:, s, e, at:at + P],
                                       lambda s: wv_s[:, s, e, half * width:(half + 1) * width],
                                       e == 0, e == EC - 1, k == 0)
                if kind in ("YT", "XT"):
                    pe.wait_ge(y_ready, Y_HALVES.after(phase, x))
                    for e in range(EC):
                        for k in range(2):
                            at = (2 * e + k) * P
                            mm = nc.tensor.transpose(bank[:, at:at + P], y[:, k, e * P:(e + 1) * P], identf[:, :])
                if kind == "FO":
                    if phase.name == "prologue":
                        pe.wait_ge(tern_ready, 1)
                    pe.wait_ge(ln_lo, FFN_OUT.after(phase, x))
                    for k in range(2):
                        for e in range(EC):
                            for s in range(2):
                                mm = nc.tensor.matmul(bank[:, k * E:(k + 1) * E], lnT[:, s, e, k * P:(k + 1) * P],
                                                      w_tern[:, e, :], start=k == 0 and e == 0 and s == 0,
                                                      stop=e == EC - 1 and s == 1, skip_group_check=True)
                mm.then_inc(job_ready, 1)

            pe.wait_ge(abs_summed, 2)
            nc.tensor.matmul(probsT_p[:, 0, 0:1], y[:, 0, 0:P], thr[:, 0:1],
                             start=True, stop=True).then_inc(scale_ready, 1)
            pe.wait_ge(rows_in, 16 * 3)
            for bank in scores_p:
                nc.tensor.matmul(bank[:, :, :], identf[:, :], identf[:, :].unsqueeze(1).to_broadcast([P, 4, P]),
                                 start=True, stop=True, skip_group_check=True).then_inc(banks_open, 1)
            for phase in passes(pe):
                for x in phase.steps(TENSOR):
                    {"S": scores, "T": transpose_probs, "W": values, "O": project}.get(x[0], job)(phase, x)

        @block.vector
        def _(dve):
            def split_low(_, x):
                n = x[1]
                where, _, _, dst = PIECES[n]
                dve.wait_ge(split_hi, n + 1)
                nc.vector.tensor_tensor(dst[1], where, dst[0].bitcast(F32), ALU.subtract).then_inc(split_lo, 1)

            def max_of(phase, x):
                i = x[1] % 2
                dve.wait_ge(scores_ready, phase.unit(x) + 1)
                nc.vector.tensor_reduce(neg_max[:, i, :], scores_p[i][:, :, :], AX.X, ALU.max,
                                        negate=True).then_inc(max_ready, 1)

            def invert_sums(phase, x):
                i = x[1] % 2
                dve.wait_ge(exp_ready, phase.unit(x) + 1)
                nc.vector.reciprocal(inv_sum[:, i, :], row_sum[:, i, :]).then_inc(inv_ready, 1)

            def heads_low(phase, x):
                g = x[1] // BLOCKS
                dve.wait_ge(heads_hi, phase.unit(x) + 1)
                nc.vector.scalar_tensor_tensor(
                    out=flat_heads(headsT[:, 1]), in0=flat_heads(heads_p[:, :]), scalar=bv_s[:, g:g + 1],
                    in1=flat_heads(headsT[:, 0]).bitcast(F32), op0=ALU.add, op1=ALU.subtract).then_inc(heads_lo, 1)

            def probsT_low(phase, x):
                dve.wait_ge(probsT_hi, phase.unit(x) + 1)
                nc.vector.tensor_tensor(probsT[:, 1, :, :], probsT_p[:, :, :].rearrange("p (c a) n -> p c (a n)", c=2),
                                        probsT[:, 0, :, :].bitcast(F32), ALU.subtract).then_inc(probsT_lo, 1)

            def rope_end(phase, x):
                x = (x[0].removeprefix("end_"), *x[1:])
                dve.wait_ge(rope_hi, ROPED.after(phase, x))
                nc.vector.tensor_tensor(roped(x, 1), as_roped(x, rope_cos[:, ROPED.parity(phase, x), :]),
                                        roped(x, 0).bitcast(F32), ALU.subtract).then_inc(rope_lo, 1)

            def rope_add(phase, x):
                x = (x[0].removeprefix("add_"), x[1], "next")
                r = ROPED.parity(phase, x)
                dve.wait_ge(rope_sined, ROPED.after(phase, x))
                dve.wait_ge(rope_cosed, ROPED.after(phase, x))
                nc.vector.tensor_tensor(rope_cos[:, r, :], rope_cos[:, r, :], rope_sin[:, r, :], ALU.add).then_inc(rope_added, 1)

            def ffn_in_low(phase, x):
                x = ("YT", *x[1:])
                dve.wait_ge(ln_hi, FFN_IN.after(phase, x))
                nc.vector.tensor_tensor(lnT[:, 1, :, :], ln_full[:, :, :], lnT[:, 0, :, :].bitcast(F32),
                                        ALU.subtract).then_inc(ln_lo, 1)

            def take(phase, x):
                kind, i, part = x
                bank = bank_of(phase, x)
                halves = "p (k n) -> p k n"
                dve.wait_ge(job_ready, BANKED.after(phase, x))
                if kind in ("Q", "K"):
                    dve.wait_ge(rope_swapped, ROPED.after(phase, x))
                    n = ROPED.before(phase, x)
                    if not (phase.name == "prologue" and n < 2):
                        dve.wait_ge(rope_lo, n - 1)
                    r = ROPED.parity(phase, x)
                    if x == ("K", 0, "next") and phase.name == "prologue":
                        dve.wait_ge(consts_in, 16 * 2)
                    bias = (bq_s if kind == "Q" else bk_s)[:, i:i + 1]
                    nc.vector.scalar_tensor_tensor(
                        out=rope_cos[:, r, :], in0=bank[:, :], scalar=bias, in1=cos_t,
                        op0=ALU.add, op1=ALU.mult).then_inc(rope_cosed, 1)
                if kind == "V":
                    dve.wait_ge(v_hi, VALUES.after(phase, x))
                    nc.vector.tensor_tensor(v_part(i, 1), bank[:, :].rearrange(halves, k=2), v_part(i, 0).bitcast(F32),
                                            ALU.subtract).then_inc(v_lo, 1)
                if kind == "XT":
                    dve.wait_ge(xn_hi, XN.after(phase, x))
                    nc.vector.tensor_tensor(xn_part(i, 1), bank[:, :].rearrange(halves, k=2),
                                            xn_part(i, 0).bitcast(F32), ALU.subtract).then_inc(xn_lo, 1)
                if kind == "YT":
                    if phase.name == "prologue" and i == 0:
                        dve.wait_ge(rows_in, 16 * 3)
                        dve.wait_ge(tern_ready, 1)
                    else:
                        dve.wait_ge(ln_lo, FFN_IN.before(phase, x))
                    for e in range(EC):
                        nc.vector.tensor_scalar(ln_full[:, e, :], bank[:, e * 2 * P:(e + 1) * 2 * P],
                                                gamma_s[:, e:e + 1], beta_s[:, e:e + 1],
                                                ALU.mult, ALU.add).then_inc(ln_scaled, 1)
                if kind == "FO":
                    src, dst = (x_res, x_res) if part == "prev" else (x_in, x_mid)
                    dve.wait_ge(biased[part], BIASED[part].after(phase, ("YT", i, part)))
                    if part == "next" and phase.has("cur"):
                        dve.wait_ge(res_ready, phase.b + 1)
                    nc.vector.scalar_tensor_tensor(
                        out=dst[:, 2 * i:2 * i + 2, :], in0=bank[:, :].rearrange(halves, k=2), scalar=0.5,
                        in1=src[:, 2 * i:2 * i + 2, :], op0=ALU.mult, op1=ALU.add).then_inc(ffn_added, 1)

            def statistics(phase, x):
                (norm, src), m = norm_of(x), x[1]
                if x[0] == "astats":
                    dve.wait_ge(ffn_added, FFN_OUT.after(phase, ("FO", m, "next")))
                elif x[2] == "prev":
                    dve.wait_ge(attn_read, 2 * phase.b - 1 + m)
                else:
                    dve.wait_ge(x_loaded[m], 16 * (phase.b + 2))
                if not (phase.name == "prologue" and norm[:2] == ("norm1", 0)):
                    dve.wait_ge(stats_ready, NORMED.before(phase, norm))
                half = slice(2 * m, 2 * m + 2)
                for k in range(2):
                    nc.vector.bn_stats(parts[:, 2 * m + k, :], src[:, 2 * m + k, :]).then_inc(parts_ready, 1)
                dve.wait_ge(parts_ready, 2 * NORMED.after(phase, norm))
                factor = variance_factor(norm)
                even, odd = parts[:, half, 0:3], parts[:, half, 3:6]
                done = 5 * NORMED.before(phase, norm)
                nc.vector.tensor_tensor(sums[:, 0, half], even[:, :, 1], odd[:, :, 1], ALU.add).then_inc(gathered, 1)
                nc.vector.tensor_tensor(sums[:, 1, half], even[:, :, 1], odd[:, :, 1], ALU.subtract).then_inc(gathered, 1)
                nc.vector.tensor_tensor(sums[:, 2, half], even[:, :, 2], odd[:, :, 2], ALU.add).then_inc(gathered, 1)
                dve.wait_ge(gathered, done + 2)
                nc.vector.tensor_scalar(stats[:, half, 0], sums[:, 0, half], 0.5, None, ALU.mult).then_inc(gathered, 1)
                nc.vector.scalar_tensor_tensor(out=sums[:, 3, half], in0=sums[:, 1, half], scalar=0.25 * factor,
                                               in1=sums[:, 1, half], op0=ALU.mult, op1=ALU.mult).then_inc(gathered, 1)
                dve.wait_ge(gathered, done + 5)
                nc.vector.scalar_tensor_tensor(out=stats[:, half, 1], in0=sums[:, 2, half], scalar=factor / E,
                                               in1=sums[:, 3, half], op0=ALU.mult, op1=ALU.add).then_inc(stats_ready, 1)

            def normalize(phase, x):
                (norm, src), m = norm_of(x), x[1]
                dve.wait_ge(rstd_ready, NORMED.after(phase, norm))
                if phase.name == "prologue" and x == ("norm", 0, "next"):
                    dve.wait_ge(scale_ready, 1)
                if x == ("anorm", 1, "next"):
                    dve.wait_ge(job_ready, BANKED.after(phase, ("XT", 0, "next")))
                for k in range(2):
                    at = 2 * m + k
                    ins = nc.vector.tensor_scalar(y[:, k, :], src[:, at, :], stats[:, at, 0:1], rstd[:, at:at + 1],
                                                  ALU.subtract, ALU.mult)
                ins.then_inc(y_ready, 1)

            def after_attention(phase, x):
                m = x[1]
                dve.wait_ge(projected, UNITS * phase.b - (0 if m else BLOCKS // 2))
                if m == 0:
                    dve.wait_ge(res_ready, phase.b)
                nc.vector.tensor_tensor(x_res[:, 2 * m:2 * m + 2, :], attn_p[m][:, :, :],
                                        x_res[:, 2 * m:2 * m + 2, :], ALU.add).then_inc(attn_read, 1)

            def ternary(_, x):
                if x[1] == 0:
                    nc.vector.memset(y[:, 0, 0:P], 1.0).then_inc(abs_summed, 1)
                    dve.wait_ge(tern_in, 16)
                    nc.vector.tensor_reduce(thr[:, 0:1], ln_full[:, :, :].rearrange("p c n -> p (c n)"), AX.X, ALU.add,
                                            apply_absolute_value=True).then_inc(abs_summed, 1)
                    return
                dve.wait_ge(scale_ready, 1)
                nc.vector.tensor_scalar(thr[:, 1:2], probsT_p[:, 0, 0:1], 1.0 / (E * E), Q_EPS,
                                        ALU.mult, ALU.add).then_inc(thr_step, 1)
                dve.wait_ge(thr_step, 1)
                nc.vector.tensor_scalar(thr[:, 2:3], thr[:, 1:2], 0.5, None, ALU.mult).then_inc(thr_step, 1)
                dve.wait_ge(thr_step, 2)
                nc.vector.tensor_scalar(x_mid[:, 0:2, :], ln_full[:, :, :], thr[:, 2:3], None,
                                        ALU.is_gt).then_inc(thr_step, 1)
                nc.vector.tensor_scalar(x_mid[:, 2:4, :], ln_full[:, :, :], -1.0, thr[:, 2:3],
                                        ALU.mult, ALU.is_gt).then_inc(thr_step, 1)
                dve.wait_ge(thr_step, 4)
                nc.vector.tensor_tensor(w_tern[:, :, :], x_mid[:, 0:2, :], x_mid[:, 2:4, :],
                                        ALU.subtract).then_inc(tern_ready, 1)

            for phase in passes(dve):
                for x in phase.steps(VECTOR):
                    {"max": max_of, "inv": invert_sums, "heads": heads_low, "probsT": probsT_low,
                     "end_Q": rope_end, "end_K": rope_end, "add_Q": rope_add, "add_K": rope_add,
                     "end_YT": ffn_in_low, "evac": after_attention, "w": split_low,
                     "stats": statistics, "astats": statistics, "norm": normalize,
                     "anorm": normalize, "tern": ternary}.get(x[0], take)(phase, x)

        @block.scalar
        def _(act):
            def split_high(_, x):
                n = x[1]
                where, s, _, dst = PIECES[n]
                act.wait_ge(staged[s], 16 * (len(staged_before(n)) + 1))
                nc.scalar.activation(dst[0], where, ACT.Copy).then_inc(split_hi, 1)

            def exp_of(phase, x):
                i = x[1] % 2
                act.wait_ge(max_ready, phase.unit(x) + 1)
                if phase.name == "first" and x[1] == 0:
                    act.wait_ge(split_lo, 4)
                for k in range(4):
                    ins = nc.scalar.activation(probs[:, i, k, :], scores_p[i][:, k, :], ACT.Exp,
                                               bias=neg_max[:, i, k:k + 1], accum_out=row_sum[:, i, k:k + 1])
                ins.then_inc(exp_ready, 1)

            def mask_bank(phase, x):
                u = phase.unit(x)
                if phase.name == "prologue":
                    act.wait_ge(consts_in, 16 * 2)
                    act.wait_ge(banks_open, x[1] + 1)
                elif not (phase.name == "first" and x[2] == "cur" and x[1] < 2):
                    act.wait_ge(exp_ready, u - 1)
                off = 0 if x[1] % BLOCKS == 0 else 2 * P
                nc.scalar.activation(scores_p[x[1] % 2][:, :, :].rearrange("p k n -> p (k n)"),
                                     mask_s[:, off:off + 4 * P], ACT.Copy).then_inc(mask_ready, 1)

            def heads_high(phase, x):
                g = x[1] // BLOCKS
                act.wait_ge(heads_ready, phase.unit(x) + 1)
                nc.scalar.activation(flat_heads(headsT[:, 0]), flat_heads(heads_p[:, :]), ACT.Identity,
                                     bias=bv_s[:, g:g + 1]).then_inc(heads_hi, 1)

            def probsT_high(phase, x):
                act.wait_ge(probsT_ready, phase.unit(x) + 1)
                nc.scalar.activation(probsT[:, 0, :, :], probsT_p[:, :, :].rearrange("p (c a) n -> p c (a n)", c=2),
                                     ACT.Copy).then_inc(probsT_hi, 1)

            def rope_end(phase, x):
                x = (x[0].removeprefix("end_"), *x[1:])
                kind, i, part = x
                act.wait_ge(rope_added, ROPED.after(phase, x))
                if phase.name == "first" and x == ("Q", GROUP, "cur"):
                    act.wait_ge(split_lo, 8)
                g = (i // GROUP if kind == "Q" else i) + (NKV if part == "next" else 0)
                if phase.has("cur") and not (phase.name == "first" and g == 1):
                    act.wait_ge(scores_ready, UNITS * phase.b + BLOCKS * (g - 1))
                nc.scalar.activation(roped(x, 0), as_roped(x, rope_cos[:, ROPED.parity(phase, x), :]),
                                     ACT.Copy).then_inc(rope_hi, 1)

            def take(phase, x):
                kind, i, part = x
                bank = bank_of(phase, x)
                halves = "p (k n) -> p k n"
                act.wait_ge(job_ready, BANKED.after(phase, x))
                if kind in ("Q", "K"):
                    r = ROPED.parity(phase, x)
                    bias = (bq_s if kind == "Q" else bk_s)[:, i:i + 1]
                    if x == ("K", 0, "next") and phase.name == "prologue":
                        act.wait_ge(consts_in, 16 * 2)
                        act.wait_ge(split_lo, 2)
                    n = ROPED.before(phase, x)
                    if not (phase.name == "prologue" and n < 2):
                        act.wait_ge(rope_added, n - 1)
                    nc.scalar.activation(rope_sin[0:HALF, r, :], bank[HALF:P, :], ACT.Identity, bias=bias[HALF:P, :])
                    nc.scalar.activation(rope_sin[HALF:P, r, :], bank[0:HALF, :], ACT.Identity,
                                         bias=bias[0:HALF, :]).then_inc(rope_swapped, 1)
                if kind == "V":
                    if i[0] == 1 and phase.has("prev"):
                        act.wait_ge(heads_ready, UNITS * phase.b)
                    if i[0] == 0 and phase.has("cur"):
                        act.wait_ge(heads_ready, UNITS * phase.b + UNITS // 2)
                    nc.scalar.activation(v_part(i, 0), bank[:, :].rearrange(halves, k=2), ACT.Copy).then_inc(v_hi, 1)
                if kind == "XT":
                    nc.scalar.activation(xn_part(i, 0), bank[:, :].rearrange(halves, k=2), ACT.Copy).then_inc(xn_hi, 1)
                if kind == "YT":
                    act.wait_ge(ln_scaled, 2 * FFN_IN.after(phase, x))
                    nc.scalar.activation(lnT[:, 0, :, :], ln_full[:, :, :], ACT.Copy).then_inc(ln_hi, 1)

            for phase in passes(act):
                for x in phase.steps(SCALAR):
                    {"exp": exp_of, "mask": mask_bank, "heads": heads_high, "probsT": probsT_high, "end_Q": rope_end,
                     "end_K": rope_end, "w": split_high}.get(x[0], take)(phase, x)

        @block.gpsimd
        def _(pool):
            def scale_of(phase, x):
                norm, _ = norm_of(x)
                half = slice(2 * x[1], 2 * x[1] + 2)
                added = eps if norm[0] == "norm_attn" else eps_twice
                pool.wait_ge(stats_ready, NORMED.after(phase, norm))
                nc.gpsimd.tensor_tensor(tmp[:, half], stats[:, half, 1], added[:, half], ALU.add).then_inc(rstd_step, 1)
                pool.wait_ge(rstd_step, NORMED.after(phase, norm))
                nc.gpsimd.tensor_tensor(rstd[:, half], tmp[:, half], minus_half[:, half], ALU.pow).then_inc(rstd_ready, 1)

            def normalize_probs(phase, x):
                i = x[1] % 2
                pool.wait_ge(inv_ready, phase.unit(x) + 1)
                nc.gpsimd.tensor_tensor(probs[:, i, :, :], probs[:, i, :, :],
                                        inv_sum[:, i, :].unsqueeze(2).to_broadcast([P, 4, P]),
                                        ALU.mult).then_inc(probs_ready, 1)

            def rope(phase, x):
                r = ROPED.parity(phase, x)
                if phase.name == "prologue" and x[:2] == ("K", 0):
                    pool.wait_ge(consts_in, 16 * 2)
                pool.wait_ge(rope_swapped, ROPED.after(phase, x))
                nc.gpsimd.tensor_tensor(rope_sin[:, r, :], rope_sin[:, r, :], sin_t, ALU.mult).then_inc(rope_sined, 1)
                if phase.name == "prologue":
                    return
                pool.wait_ge(rope_sined, ROPED.after(phase, x))
                pool.wait_ge(rope_cosed, ROPED.after(phase, x))
                nc.gpsimd.tensor_tensor(rope_cos[:, r, :], rope_cos[:, r, :], rope_sin[:, r, :], ALU.add).then_inc(rope_added, 1)

            def bias_residual(phase, x):
                _, m, part = x
                buf = x_res if part == "prev" else x_in
                pool.wait_ge(y_ready, Y_HALVES.after(phase, ("YT", m, part)))
                nc.gpsimd.tensor_tensor(buf[:, 2 * m:2 * m + 2, :], buf[:, 2 * m:2 * m + 2, :],
                                        half_b.unsqueeze(1).to_broadcast([P, 2, E]), ALU.add).then_inc(biased[part], 1)

            def halve_bias(_, x):
                pool.wait_ge(rows_in, 16 * 3)
                nc.gpsimd.tensor_scalar(half_b, half_b, 0.5, None, ALU.mult).then_inc(bias_ready, 1)
                pool.wait_ge(bias_ready, 1)

            def residual(phase, _):
                if phase.has("prev"):
                    pool.wait_ge(out_stored, 2 * 16 * phase.b)
                else:
                    pool.wait_ge(split_lo, len(PIECES))
                    pool.wait_ge(ffn_added, FFN_OUT.start(phase))
                nc.gpsimd.tensor_tensor(x_res[:, :, :], x_mid[:, :, :],
                                        bo_t.unsqueeze(1).to_broadcast([P, BLOCKS, E]), ALU.add).then_inc(res_ready, 1)

            nc.gpsimd.memset(minus_half[:, :], -0.5).then_inc(power_ready, 1)
            nc.gpsimd.memset(eps[:, :], LN_EPS).then_inc(power_ready, 1)
            nc.gpsimd.memset(eps_twice[:, :], LN_EPS * LN_EPS).then_inc(power_ready, 1)
            pool.wait_ge(power_ready, 3)
            for phase in passes(pool):
                for x in phase.steps(GPSIMD):
                    {"probs": normalize_probs, "scale": scale_of, "ascale": scale_of, "bias": bias_residual,
                     "residual": residual, "half": halve_bias}.get(x[0], rope)(phase, x)


def constants():
    half = np.arange(HALF, dtype=np.float32)
    freqs = np.float32(1.0) / np.float32(ROPE_BASE) ** (np.float32(2.0) * half / np.float32(HD))
    angles = (np.arange(SEQ, dtype=np.float32)[:, None] * freqs[None, :]).astype(np.float32).T.astype(np.float64)
    scale = float(HD) ** -0.25
    cosT = (np.concatenate([np.cos(angles)] * 2) * scale).astype(np.float32)
    sinT = (np.concatenate([-np.sin(angles), np.sin(angles)]) * scale).astype(np.float32)
    q = np.arange(P)[:, None] % CHUNK
    key = np.arange(P)[None, :]
    windowed = (key - CHUNK <= q) & (q - (key - CHUNK) <= WINDOW)
    causal = key <= q
    mask = np.concatenate([causal] * 2 + [windowed] * 4, axis=1)
    return cosT, sinT, np.where(mask, 0.0, MASKED), np.eye(P)


def kernel(L0_attn_x, L0_attn_Wq, L0_attn_bq, L0_attn_Wk, L0_attn_bk, L0_attn_Wv, L0_attn_bv, L0_attn_Wo,
           L0_attn_bo, L0_ffn_weight, L0_ffn_bias, L0_ffn_ln_gamma, L0_ffn_ln_beta):
    import ml_dtypes
    import concourse.bacc as bacc
    from concourse.bass_utils import run_bass_kernel_spmd

    def evens_first(w):
        w = np.asarray(w)
        heads = w.reshape(*w.shape[:-1], -1, HALF, 2)
        return np.ascontiguousarray(np.swapaxes(heads, -1, -2).reshape(w.shape))

    def by_head(b):
        return np.ascontiguousarray(np.asarray(b).reshape(-1, HD).T)

    cosT, sinT, mask, eye = constants()
    arrays = {
        "x": np.ascontiguousarray(L0_attn_x),
        "wq": evens_first(L0_attn_Wq), "wk": evens_first(L0_attn_Wk),
        "wv": np.ascontiguousarray(L0_attn_Wv), "wo": np.ascontiguousarray(L0_attn_Wo),
        "ffn_wT": np.ascontiguousarray(np.asarray(L0_ffn_weight).T),
        "columns": np.concatenate([by_head(evens_first(L0_attn_bq)), by_head(evens_first(L0_attn_bk)),
                                   by_head(L0_attn_bv), by_head(L0_ffn_ln_gamma), by_head(L0_ffn_ln_beta)], axis=1),
        "rows": np.stack([np.asarray(L0_ffn_bias), np.asarray(L0_attn_bo)]),
        "rope_tables": np.stack([cosT, sinT], axis=1), "mask": mask.astype(ml_dtypes.bfloat16),
        "ident": eye.astype(np.float32),
    }
    nc = bacc.Bacc("TRN2", target_bir_lowering=False, num_devices=1)
    args = [nc.dram_tensor(name, a.shape, mybir.dt.from_np(a.dtype), kind="ExternalInput").ap()
            for name, a in arrays.items()]
    out = nc.dram_tensor("out", (BATCHES, SEQ, E), F32, kind="ExternalOutput").ap()
    block_kernel(nc, *args, out)
    r = run_bass_kernel_spmd(nc, [arrays], core_ids=[0])
    return r.results[0]["out"]
```
